# Optimizing a Trainium2 kernel written in Bass

```python
import numpy as np
import jax
import jax.numpy as jnp

def _softmax(x, axis=-1):
    return jax.nn.softmax(x, axis=axis)

def _gelu(x):
    return jax.nn.gelu(x, approximate=True)

def _silu(x):
    return jax.nn.silu(x)

def _sigmoid(x):
    return jax.nn.sigmoid(x)

def _layernorm(x, axis=-1, eps=1e-05):
    m = jnp.mean(x, axis=axis, keepdims=True)
    v = jnp.var(x, axis=axis, keepdims=True)
    return (x - m) / jnp.sqrt(v + eps)

def _scatter_add(tgt, idx, src, axis=0):
    return tgt.at[idx].add(src)

def _segment_sum(src, seg, n):
    return jax.ops.segment_sum(src, seg, n)
kernel_name = 'mk_xattn_ffn_d1_seqx_r8_82120a'

def setup_inputs(seed: int=0):
    np.random.seed(seed)
    _w = jnp.asarray

    def _rec_inputs():
        import jax
        import jax.numpy as jnp
        _rk = jax.random.key(seed)
        x = 7.22e-05 + 1 * jax.random.normal(jax.random.fold_in(_rk, 1), (32, 64, 256), jnp.float32)
        _lenS = 64 - jax.random.randint(jax.random.fold_in(_rk, 7), (32,), 0, max(1, 64 // 4) + 1, jnp.int32)
        _lenS2 = 64 - jax.random.randint(jax.random.fold_in(_rk, 8), (32,), 0, max(1, 64 // 4) + 1, jnp.int32)
        _ctx_1024P = jax.random.normal(jax.random.fold_in(_rk, 11), (32, 16, 128), jnp.float32)
        _ctx_1024c = jax.random.dirichlet(jax.random.fold_in(_rk, 511), 0.3 * jnp.ones((16,), jnp.float32), (32, 64))
        _ctx_1024t = jnp.einsum('bsk,bkd->bsd', _ctx_1024c, _ctx_1024P)
        _ctx_1024t = _ctx_1024t * jax.lax.rsqrt(jnp.mean(jnp.square(_ctx_1024t)) + 1e-12) * 0.953939
        ctx_1024 = -0.000673644 + 1.00013 * (_ctx_1024t + 0.3 * jax.random.normal(jax.random.fold_in(_rk, 611), (32, 64, 128), jnp.float32))
        return (x, ctx_1024)
    x, ctx_1024 = _rec_inputs()

    def _L0_xattn_setup():
        import jax, jax.numpy as jnp
        import numpy as np
        B, S1, S2, DCA = (2, 256, 128, 16)
        QDIM, KDIM, H = (256, 128, 16)
        HD = QDIM // H
        SCALE = HD ** (-0.5)
        EPS = 1e-06
        DCA_WEIGHT = 1.0

        def _ln(t, w, b):
            m = jnp.mean(t, axis=-1, keepdims=True)
            v = jnp.var(t, axis=-1, keepdims=True)
            return (t - m) * jax.lax.rsqrt(v + EPS) * w + b

        def _attn(q, k, v):
            s = jnp.einsum('bhqd,bhkd->bhqk', q, k) * SCALE
            p = jax.nn.softmax(s, axis=-1)
            return jnp.einsum('bhqk,bhkd->bhqd', p, v)
        key = jax.random.key(seed)
        ks = jax.random.split(key, 8)
        w = lambda k, shape: jax.random.normal(k, shape, jnp.float32) * 0.02
        return {'x': jax.random.normal(ks[0], (B, S1, QDIM), jnp.float32), 'y': jax.random.normal(ks[1], (B, S2 + DCA, KDIM), jnp.float32), 'Wq': w(ks[2], (QDIM, QDIM)), 'bq': jnp.zeros((QDIM,), jnp.float32), 'Wk': w(ks[3], (KDIM, QDIM)), 'bk': jnp.zeros((QDIM,), jnp.float32), 'Wv': w(ks[4], (KDIM, QDIM)), 'bv': jnp.zeros((QDIM,), jnp.float32), 'Wkv_dca': w(ks[5], (KDIM, 2 * QDIM)), 'bkv_dca': jnp.zeros((2 * QDIM,), jnp.float32), 'qn_w': jnp.ones((HD,), jnp.float32), 'qn_b': jnp.zeros((HD,), jnp.float32), 'kn_w': jnp.ones((HD,), jnp.float32), 'kn_b': jnp.zeros((HD,), jnp.float32), 'kn_dca_w': jnp.ones((HD,), jnp.float32), 'kn_dca_b': jnp.zeros((HD,), jnp.float32), 'Wo': w(ks[6], (QDIM, QDIM)), 'bo': jnp.zeros((QDIM,), jnp.float32)}
    _L0_xattn_all = _L0_xattn_setup()
    _L0_xattn_in = {k: v for k, v in _L0_xattn_all.items() if k in ('Wq', 'bq', 'Wk', 'bk', 'Wv', 'bv', 'Wkv_dca', 'bkv_dca', 'qn_w', 'qn_b', 'kn_w', 'kn_b', 'kn_dca_w', 'kn_dca_b', 'Wo', 'bo')}
    del _L0_xattn_all

    def _L0_ffn_setup():
        import jax
        import jax.numpy as jnp
        import numpy as np
        NUM_EXPERTS = 32
        HIDDEN = 256
        INTER = 96
        TOP_K = 8
        TAU = 0.05
        BATCH, SEQ = (2, 128)
        key = jax.random.key(seed)
        k1, k2, k3, k4 = jax.random.split(key, 4)
        return {'hidden_states': jax.random.normal(k1, (BATCH, SEQ, HIDDEN), dtype=jnp.float32), 'gate_weight': jax.random.normal(k2, (NUM_EXPERTS, HIDDEN), dtype=jnp.float32) * 0.02, 'gate_up_proj': jax.random.normal(k3, (NUM_EXPERTS, 2 * INTER, HIDDEN), dtype=jnp.float32) * 0.02, 'down_proj': jax.random.normal(k4, (NUM_EXPERTS, HIDDEN, INTER), dtype=jnp.float32) * 0.02, 'layer_alpha': jnp.array(1.0, dtype=jnp.float32)}
    _L0_ffn_all = _L0_ffn_setup()
    _L0_ffn_in = {k: v for k, v in _L0_ffn_all.items() if k in ('gate_weight', 'gate_up_proj', 'down_proj', 'layer_alpha')}
    del _L0_ffn_all
    return {'x': x, 'ctx_1024': ctx_1024, 'L0_xattn_Wq': _L0_xattn_in['Wq'], 'L0_xattn_bq': _L0_xattn_in['bq'], 'L0_xattn_Wk': _L0_xattn_in['Wk'], 'L0_xattn_bk': _L0_xattn_in['bk'], 'L0_xattn_Wv': _L0_xattn_in['Wv'], 'L0_xattn_bv': _L0_xattn_in['bv'], 'L0_xattn_Wkv_dca': _L0_xattn_in['Wkv_dca'], 'L0_xattn_bkv_dca': _L0_xattn_in['bkv_dca'], 'L0_xattn_qn_w': _L0_xattn_in['qn_w'], 'L0_xattn_qn_b': _L0_xattn_in['qn_b'], 'L0_xattn_kn_w': _L0_xattn_in['kn_w'], 'L0_xattn_kn_b': _L0_xattn_in['kn_b'], 'L0_xattn_kn_dca_w': _L0_xattn_in['kn_dca_w'], 'L0_xattn_kn_dca_b': _L0_xattn_in['kn_dca_b'], 'L0_xattn_Wo': _L0_xattn_in['Wo'], 'L0_xattn_bo': _L0_xattn_in['bo'], 'L0_ffn_gate_weight': _L0_ffn_in['gate_weight'], 'L0_ffn_gate_up_proj': _L0_ffn_in['gate_up_proj'], 'L0_ffn_down_proj': _L0_ffn_in['down_proj'], 'L0_ffn_layer_alpha': _L0_ffn_in['layer_alpha']}

def reference(x, ctx_1024, L0_xattn_Wq, L0_xattn_bq, L0_xattn_Wk, L0_xattn_bk, L0_xattn_Wv, L0_xattn_bv, L0_xattn_Wkv_dca, L0_xattn_bkv_dca, L0_xattn_qn_w, L0_xattn_qn_b, L0_xattn_kn_w, L0_xattn_kn_b, L0_xattn_kn_dca_w, L0_xattn_kn_dca_b, L0_xattn_Wo, L0_xattn_bo, L0_ffn_gate_weight, L0_ffn_gate_up_proj, L0_ffn_down_proj, L0_ffn_layer_alpha):
    import jax
    import jax.numpy as jnp

    def _L0_xattn_ref(x, y, Wq, bq, Wk, bk, Wv, bv, Wkv_dca, bkv_dca, qn_w, qn_b, kn_w, kn_b, kn_dca_w, kn_dca_b, Wo, bo):
        import jax, jax.numpy as jnp
        import numpy as np
        B, S1, S2, DCA = (2, 256, 128, 16)
        QDIM, KDIM, H = (256, 128, 16)
        HD = QDIM // H
        SCALE = HD ** (-0.5)
        EPS = 1e-06
        DCA_WEIGHT = 1.0

        def _ln(t, w, b):
            m = jnp.mean(t, axis=-1, keepdims=True)
            v = jnp.var(t, axis=-1, keepdims=True)
            return (t - m) * jax.lax.rsqrt(v + EPS) * w + b

        def _attn(q, k, v):
            s = jnp.einsum('bhqd,bhkd->bhqk', q, k) * SCALE
            p = jax.nn.softmax(s, axis=-1)
            return jnp.einsum('bhqk,bhkd->bhqd', p, v)
        b, s1, _ = x.shape
        y_dca = y[:, -DCA:, :]
        y_main = y[:, :-DCA, :]
        kv_dca = (y_dca @ Wkv_dca + bkv_dca).reshape(b, DCA, 2, H, HD)
        k_dca = _ln(kv_dca[:, :, 0], kn_dca_w, kn_dca_b)
        v_dca = kv_dca[:, :, 1]
        s2 = y_main.shape[1]
        q = _ln((x @ Wq + bq).reshape(b, s1, H, HD), qn_w, qn_b)
        kv = jnp.concatenate([y_main @ Wk + bk, y_main @ Wv + bv], axis=-1)
        kv = kv.reshape(b, s2, H, 2 * HD)
        k = _ln(kv[..., :HD], kn_w, kn_b)
        v = kv[..., HD:]
        qT = q.transpose(0, 2, 1, 3)
        ctx = _attn(qT, k.transpose(0, 2, 1, 3), v.transpose(0, 2, 1, 3))
        ctx = ctx.transpose(0, 2, 1, 3).reshape(b, s1, QDIM)
        ctx_dca = _attn(qT, k_dca.transpose(0, 2, 1, 3), v_dca.transpose(0, 2, 1, 3))
        ctx_dca = ctx_dca.transpose(0, 2, 1, 3).reshape(b, s1, QDIM)
        ctx = ctx + DCA_WEIGHT * ctx_dca
        return ctx @ Wo + bo

    def _L0_ffn_ref(hidden_states, gate_weight, gate_up_proj, down_proj, layer_alpha):
        import jax
        import jax.numpy as jnp
        import numpy as np
        NUM_EXPERTS = 32
        HIDDEN = 256
        INTER = 96
        TOP_K = 8
        TAU = 0.05
        BATCH, SEQ = (2, 128)
        B, S, H = hidden_states.shape
        x = hidden_states.reshape(-1, H)
        T = x.shape[0]
        logits = x @ gate_weight.T
        probs = jax.nn.softmax(logits.astype(jnp.float32), axis=-1).astype(logits.dtype)
        topv, topi = jax.lax.top_k(probs, TOP_K)
        topv = topv / jnp.clip(topv.sum(axis=-1, keepdims=True), 1e-12)
        scaled = topv * layer_alpha.astype(topv.dtype)
        active = scaled >= TAU
        empty = ~jnp.any(active, axis=-1)
        fallback = jnp.arange(TOP_K)[None, :] == jnp.argmax(scaled, axis=-1)[:, None]
        active = active | empty[:, None] & fallback
        routing_weights = topv * active.astype(topv.dtype)
        routing_weights = routing_weights / jnp.clip(routing_weights.sum(axis=-1, keepdims=True), 1e-12)
        combine = jnp.zeros((T, NUM_EXPERTS), dtype=x.dtype)
        combine = combine.at[jnp.arange(T)[:, None], topi].add(routing_weights)

        def expert_step(acc, xs):
            w_gu, w_d, c_e = xs
            gu = x @ w_gu.T
            g, u = jnp.split(gu, 2, axis=-1)
            h = jax.nn.silu(g) * u
            acc = acc + h @ w_d.T * c_e[:, None]
            return (acc, None)
        out, _ = jax.lax.scan(expert_step, jnp.zeros_like(x), (gate_up_proj, down_proj, combine.T))
        return out.reshape(B, S, H)
    x = x + _L0_xattn_ref(_layernorm(x, axis=-1), ctx_1024, L0_xattn_Wq, L0_xattn_bq, L0_xattn_Wk, L0_xattn_bk, L0_xattn_Wv, L0_xattn_bv, L0_xattn_Wkv_dca, L0_xattn_bkv_dca, L0_xattn_qn_w, L0_xattn_qn_b, L0_xattn_kn_w, L0_xattn_kn_b, L0_xattn_kn_dca_w, L0_xattn_kn_dca_b, L0_xattn_Wo, L0_xattn_bo)
    x = x + _L0_ffn_ref(_layernorm(x, axis=-1), L0_ffn_gate_weight, L0_ffn_gate_up_proj, L0_ffn_down_proj, L0_ffn_layer_alpha)
    return x

_drawn_inputs = setup_inputs


def setup_inputs(seed=0):
    import zlib

    import numpy as np

    out = dict(_drawn_inputs(seed))
    spreads = {'L0_xattn_bq': (0.0, 0.8),
     'L0_xattn_bk': (0.0, 0.401),
     'L0_xattn_bv': (0.0, 0.33),
     'L0_xattn_bkv_dca': (0.0, 0.1),
     'L0_xattn_qn_w': (1.0, 0.6),
     'L0_xattn_qn_b': (0.0, 0.8),
     'L0_xattn_kn_w': (1.0, 0.6),
     'L0_xattn_kn_b': (0.0, 0.8),
     'L0_xattn_kn_dca_w': (1.0, 0.6),
     'L0_xattn_kn_dca_b': (0.0, 0.8),
     'L0_xattn_bo': (0.0, 0.1)}
    factors = {'L0_ffn_gate_weight': 8.0, 'L0_ffn_gate_up_proj': 8.0, 'L0_ffn_down_proj': 8.0}
    for name, (base, spread) in spreads.items():
        noise = np.random.default_rng([zlib.crc32(name.encode()), seed]).standard_normal(out[name].shape)
        drawn = base * np.exp(spread * noise) if base else spread * noise
        out[name] = jnp.asarray(drawn.astype(out[name].dtype))
    for name, factor in factors.items():
        out[name] = (out[name] * factor).astype(out[name].dtype)
    return out
```

```python
import numpy as np

import concourse.bass as bass
from concourse import mybir
from concourse.bass import ds

F32 = mybir.dt.float32
F32R = mybir.dt.float32r
ALU = mybir.AluOpType
ACT = mybir.ActivationFunctionType
AX = mybir.AxisListType.X

P = 128
BATCH, SEQ, D = 32, 64, 256
TOKENS = BATCH * SEQ
CTX, DCA = 128, 16
MAIN = SEQ - DCA
HEADS, HD = 16, 16
HC = HEADS // 2
EXPERTS, INTER, TOP_K = 32, 96, 8
TAU = 0.05
LN_EPS, HEAD_EPS = 1e-5, 1e-6
GROUP = 512
GROUPS = TOKENS // GROUP
PAIRS = GROUP // P
KC = D // P
CHUNKS = EXPERTS * INTER // P
SLOTS = 3
CREDIT = 3
LAG = 2

W_Q, W_KM, W_KD, W_VM, W_VD, W_O, W_G, W_END = 0, 512, 768, 1024, 1280, 1536, 2048, 2112
B_Q, B_K, B_V, B_O = 0, 256, 512, 768
C_ID, C_KMASK, C_ALL, C_KIND, C_IOTA, C_END = 0, 128, 136, 264, 392, 424
PAR_QW, PAR_QB, PAR_KW, PAR_KB, PAR_DW, PAR_DB, PAR_ALPHA, PAR_END = 0, 1, 2, 3, 4, 5, 6, 7


def build(nc, x, yT, w_attn, b_attn, consts, params, w_up, w_down, out, c_dram):
    place = [nc.sbuf_base + (-nc.sbuf_base) % 64]
    top = nc.sbuf_usable_end

    def at(cursor, name, shape, dt=F32):
        size = int(np.prod(shape[1:])) * 4
        t = nc.alloc_sbuf_tensor_at(name, shape, dt, offset=cursor[0])
        cursor[0] += size + (-size) % 32
        assert cursor[0] <= top, (name, cursor[0], top)
        return t

    x2_hi = at(place, "x2_hi", [P, KC, TOKENS], F32R)
    x2_lo = at(place, "x2_lo", [P, KC, TOKENS], F32R)
    x1 = at(place, "x1", [P, GROUPS * PAIRS, D])
    lo_at = [place[0]]
    up_raw = at(place, "up_raw", [P, CHUNKS, KC, 2, P])
    up_lo = at(lo_at, "up_lo", [P, CHUNKS, KC, 2, P], F32R)
    con = at(place, "con", [P, C_END])
    ident = con[:, C_ID:C_ID + P]

    a1 = [place[0]]
    w_hi = at(a1, "w_hi", [P, W_END], F32R)
    w_lo = at(a1, "w_lo", [P, W_END], F32R)
    b_rows = at(a1, "b_rows", [P, 4 * D], F32R)
    ones_all = at(a1, "ones_all", [P, P], F32R)
    ones_kind = at(a1, "ones_kind", [P, P], F32R)
    par = at(a1, "par", [P, PAR_END])
    y_raw = at(a1, "y_raw", [P, TOKENS])
    y_hi = [at(a1, f"y_hi{i}", [P, PAIRS, 3, SEQ], F32R) for i in range(2)]
    y_lo = [at(a1, f"y_lo{i}", [P, PAIRS, 3, SEQ], F32R) for i in range(2)]
    f_hi = at(a1, "f_hi", [P, KC, GROUP], F32R)
    f_lo = at(a1, "f_lo", [P, KC, GROUP], F32R)
    qn = at(a1, "qn", [P, PAIRS, D])
    kn = at(a1, "kn", [P, PAIRS, D])
    qT = at(a1, "qT", [P, KC, GROUP])
    kT = at(a1, "kT", [P, KC, GROUP])
    raw_at = [a1[0]]
    k_diag = [at(a1, f"k_diag{i}", [P, KC, 2, HC, SEQ]) for i in range(2)]
    w_raw = at(raw_at, "w_raw", [P, W_END])
    b_raw = at(raw_at, "b_raw", [P, 4 * D])
    prob = [at(a1, f"prob{i}", [P, HEADS, SEQ]) for i in range(2)]
    pT = [at(a1, f"pT{i}", [P, HC, P]) for i in range(2)]
    v_diag = at(a1, "v_diag", [P, 8, HC, 2, HD])
    xn = pT[0][:].rearrange("p a b -> p (a b)").rearrange("p (a b) -> p a b", b=D)
    st = at(a1, "st", [P, PAIRS, 6])
    mv = at(a1, "mv", [P, PAIRS, 2])
    eps = at(a1, "eps", [P, 2])
    ss = at(a1, "ss", [P, 2 * PAIRS * HEADS])
    nw = at(a1, "nw", [P, 4, PAIRS * HEADS])
    rs = at(a1, "rs", [P, 2, PAIRS * HEADS])
    mx = at(a1, "mx", [P, 2, 2, HEADS])
    sm = at(a1, "sm", [P, 2, 2, HEADS])
    mean_w = mx[:, 0].rearrange("p a b -> p (a b)")
    rt = prob[0][:].rearrange("p h s -> p (h s)").rearrange("p (t a e) -> p t a e", a=PAIRS, e=EXPERTS)
    r8 = at(a1, "r8", [P, 2, PAIRS, TOP_K])
    r1 = at(a1, "r1", [P, 10, PAIRS])
    c_sb = rt[0:EXPERTS, 0:4, :, :].rearrange("p a b c -> p (a b c)")

    a2 = [place[0]]
    up_hi = at(a2, "up_hi", [P, CHUNKS, KC, 2, P], F32R)
    hid = [at(a2, f"hid{i}", [P, GROUP]) for i in range(SLOTS)]
    h_hi = [at(a2, f"h_hi{i}", [P, GROUP], F32R) for i in range(2)]
    h_lo = [at(a2, f"h_lo{i}", [P, GROUP], F32R) for i in range(2)]
    cb = [at(a2, f"cb{i}", [P, GROUP]) for i in range(SLOTS)]
    dn_raw = [at(a2, f"dn_raw{i}", [P, D]) for i in range(SLOTS)]
    dn_hi = [at(a2, f"dn_hi{i}", [P, D], F32R) for i in range(SLOTS)]
    dn_lo = [at(a2, f"dn_lo{i}", [P, D], F32R) for i in range(SLOTS)]
    acc_sb = at(a2, "acc_sb", [P, KC, GROUP])
    y_out = at(a2, "y_out", [P, PAIRS, D])

    ps = [nc.alloc_psum_tensor(f"ps{i}", [P, 2, 512], F32) for i in range(4)]
    bank = [ps[i // 2][:, i % 2, :] for i in range(8)]
    T2, Q2, K2, S2 = ps

    PER = dict(
        x_in=16, var1=1, seed1=1, xn=4, xT=2, x_hi=2, x_lo=2, y_hi=2, y_lo=2, q=2, k=2,
        q_sq=2, k_sq=2, ssq=2, seed2=2, qn=2, kn=2, qT=2, kT=2, qT_sb=2, kT_sb=4, k_diag=4, v=4, v_diag=4,
        s=4, s_sub=4, s_exp=4, s_rcp=4, prob=4, pT=8, pT_sb=8, ctx=4, c_hi=2, c_lo=2, o=2, var2=1,
        seed3=1, xn2=4, x2T=2, x2_hi=2, x2_lo=2, logit=1, l_sub=1, l_exp=1, comb=1, cT=1, c_sb=1, c_out=16, keep=32,
        dve=0,
    )
    sems = {n: nc.alloc_semaphore(f"s_{n}") for n in PER}
    s_const, s_w, s_centred, s_split_w, s_zero_y, s_zero_b, s_raw, s_ln, s_hold = (
        nc.alloc_semaphore(n) for n in
        ("s_const", "s_w", "s_centred", "s_split_w", "s_zero_y", "s_zero_b", "s_raw", "s_ln", "s_hold"))
    DVE_LINKS = 62
    LN_PER = 4

    AHEAD = ("v", "s", "s_sub", "ctx", "c_lo", "var2", "x2_lo", "cT", "c_sb", "c_out", "keep")

    def per_group(engine, g):
        def wait(name, n):
            assert n or name in AHEAD
            engine.wait_ge(sems[name], g * PER[name] + n + (name in AHEAD))
        return wait

    def splits(hi, lo):
        return ((hi, 0), (hi, 1), (lo, 0))

    with nc.Block() as block:

        @block.sync
        def _(sp):
            for name in AHEAD:
                sp.sem_inc(sems[name], 1)
            sp.dma_start(con[:], consts).then_inc(s_const, 16)
            sp.dma_start(par[:], params).then_inc(s_const, 16)
            sp.dma_start(x1[:, 0:PAIRS, :], x[:, 0:PAIRS, :]).then_inc(sems["x_in"], 16)
            sp.dma_start(y_raw[:], yT).then_inc(s_const, 16)
            for g in range(1, GROUPS):
                sp.wait_ge(sems["x_in"], 16 * g)
                sp.dma_start(x1[:, g * PAIRS:(g + 1) * PAIRS, :], x[:, g * PAIRS:(g + 1) * PAIRS, :])\
                    .then_inc(sems["x_in"], 16)
            for i in range(4):
                n = CHUNKS // 4
                sp.dma_start(up_raw[:, i * n:(i + 1) * n], w_up[:, i * n:(i + 1) * n]).then_inc(s_raw, 16)
            with sp.Fori(0, GROUPS) as g:
                wait = per_group(sp, g)
                wait("x2_lo", 2)
                for keep, part in ((x2_hi, f_hi), (x2_lo, f_lo)):
                    sp.dma_start(keep[:].bitcast(F32)[:, :, ds(g * GROUP, GROUP)], part[:].bitcast(F32)).then_inc(sems["keep"], 16)
                wait("c_sb", 1)
                sp.dma_start(c_dram[:, ds(g * GROUP, GROUP)], c_sb).then_inc(sems["c_out"], 16)
            sp.wait_ge(sems["c_out"], 16 * GROUPS + 1)
            sp.wait_ge(sems["keep"], 32 * GROUPS + 1)

        @block.gpsimd
        def _(pool):
            G = nc.gpsimd
            G.memset(v_diag[:], 0.0)
            for t in (*y_hi, *y_lo):
                last = G.memset(t[:].bitcast(F32), 0.0)
            last.then_inc(s_zero_y, 1)
            pool.wait_ge(s_zero_y, 1)
            pool.wait_ge(s_const, 48)
            kmask = con[:, C_KMASK:C_KMASK + HC]
            with pool.Fori(0, GROUPS) as g:
                wait = per_group(pool, g)
                wait("v", 0)
                y = y_raw[:, ds(g * GROUP, GROUP)].rearrange("p (a b s) -> p a b s", b=2, s=SEQ)
                for i, (a, b) in enumerate(((0, MAIN), (MAIN, SEQ))):
                    wait("y_hi", i + 1)
                    for t, n in ((0, 2), (2, 1)):
                        ins = G.tensor_tensor(y_lo[i][:, :, t:t + n, a:b], y[:, :, 0:n, a:b],
                                              y_hi[i][:, :, t:t + n, a:b].bitcast(F32), ALU.subtract)
                    ins.then_inc(sems["y_lo"], 1)

                def diagonal(p):
                    if p == 0:
                        wait("kT_sb", 4)
                        wait("s", 0)
                    if p >= 2:
                        wait("s", p - 1)
                    for c in range(KC):
                        src = kT[:, c, p * P:(p + 1) * P].rearrange("p (b o s) -> p b o s", b=2, o=1)
                        for b in range(2):
                            ins = G.tensor_tensor(k_diag[p % 2][:, c, b, :, :],
                                                  src[:, b, :, :].broadcast_to([P, HC, SEQ]),
                                                  kmask.unsqueeze(2).broadcast_to([P, HC, SEQ]), ALU.mult)
                    ins.then_inc(sems["k_diag"], 1)

                def normalise(p):
                    wait("s_rcp", p + 1)
                    for i, (a, b) in enumerate(((0, MAIN), (MAIN, SEQ))):
                        t = prob[p % 2][:, :, a:b]
                        ins = G.tensor_tensor(t, t, sm[:, p % 2, i, :].unsqueeze(2).broadcast_to([P, HEADS, b - a]),
                                              ALU.mult)
                    ins.then_inc(sems["prob"], 1)

                diagonal(0)
                diagonal(1)
                normalise(0)
                diagonal(2)
                normalise(1)
                diagonal(3)
                normalise(2)
                normalise(3)

        @block.scalar
        def _(act):
            A = nc.scalar
            act.dma_start(w_raw[:], w_attn).then_inc(s_w, 16)
            act.wait_ge(s_zero_b, 2)
            for r in range(4):
                act.dma_start(b_raw[32 * r:32 * r + 1, :], b_attn[r // 2:r // 2 + 1, :]).then_inc(s_w, 16)
            A.preload_act_table_set("natural_log_exp_and_others")
            act.wait_ge(s_centred, 1)
            A.activation(w_hi[:], w_raw[:], ACT.Copy).then_inc(s_split_w, 1)
            A.activation(b_rows[:], b_raw[:], ACT.Copy).then_inc(s_split_w, 1)
            act.wait_ge(s_const, 48)
            A.activation(ones_all[:], con[:, C_ALL:C_ALL + P], ACT.Copy).then_inc(s_split_w, 1)
            A.activation(ones_kind[:], con[:, C_KIND:C_KIND + P], ACT.Copy).then_inc(s_split_w, 1)
            act.wait_ge(s_zero_y, 1)
            with act.Fori(0, GROUPS) as g:
                wait = per_group(act, g)
                lns = [0]

                def seed(src, tmp, dst, scale, eps_col, name):
                    A.activation(tmp, src, ACT.Ln, scale=scale, bias=eps[:, eps_col:eps_col + 1])\
                        .then_inc(s_ln, 1)
                    lns[0] += 1
                    act.wait_ge(s_ln, g * LN_PER + lns[0])
                    A.activation(dst, tmp, ACT.Exp, scale=-0.5).then_inc(sems[name], 1)

                y = y_raw[:, ds(g * GROUP, GROUP)].rearrange("p (a b s) -> p a b s", b=2, s=SEQ)
                wait("v", 0)
                for i, (a, b) in enumerate(((0, MAIN), (MAIN, SEQ))):
                    for t, n in ((0, 2), (2, 1)):
                        ins = A.activation(y_hi[i][:, :, t:t + n, a:b], y[:, :, 0:n, a:b], ACT.Copy)
                    ins.then_inc(sems["y_hi"], 1)
                wait("var1", 1)
                seed(mv[:, :, 1], nw[:, 0, 0:PAIRS], rs[:, 0, 0:PAIRS], 1.0, 0, "seed1")
                wait("keep", 0)
                for c in range(KC):
                    wait("xT", c + 1)
                    A.activation(f_hi[:, c, :], T2[:, c, :], ACT.Copy).then_inc(sems["x_hi"], 1)
                wait("cT", 0)
                wait("c_out", 0)
                for i, (src, name) in enumerate(((Q2, "q"), (K2, "k"))):
                    for j in range(2):
                        wait(name, j + 1)
                        sq = prob[i][:].rearrange("p h s -> p (h s)")[:, j * 512:(j + 1) * 512]
                        A.activation(sq, src[:, j, :], ACT.Square).then_inc(sems[name + "_sq"], 1)
                    wait("ssq", i + 1)
                    n = PAIRS * HEADS
                    seed(ss[:, i * n:(i + 1) * n], nw[:, 0, :], rs[:, i, :], 1.0 / HD, 1, "seed2")
                for c in range(KC):
                    wait("qT", c + 1)
                    A.activation(qT[:, c, :], T2[:, c, :], ACT.Identity, scale=par[:, PAR_QW:PAR_QW + 1],
                                 bias=par[:, PAR_QB:PAR_QB + 1]).then_inc(sems["qT_sb"], 1)
                for c in range(KC):
                    wait("kT", c + 1)
                    for a, b, w in ((0, MAIN, PAR_KW), (MAIN, SEQ, PAR_DW)):
                        A.activation(kT[:, c, :].rearrange("p (b s) -> p b s", s=SEQ)[:, :, a:b],
                                     S2[:, c, :].rearrange("p (b s) -> p b s", s=SEQ)[:, :, a:b],
                                     ACT.Identity, scale=par[:, w:w + 1], bias=par[:, w + 1:w + 2])\
                            .then_inc(sems["kT_sb"], 1)

                def exps(p):
                    wait("s_sub", p + 1)
                    t = prob[p % 2][:].rearrange("p h s -> p (h s)")
                    A.activation(t, t, ACT.Exp, scale=HD ** -0.5).then_inc(sems["s_exp"], 1)

                def copy_pT(p):
                    if p >= 2:
                        wait("ctx", p - 1)
                    for j in range(2):
                        wait("pT", 2 * p + j + 1)
                        A.activation(pT[p % 2][:, 4 * j:4 * j + 4, :].rearrange("p a b -> p (a b)"),
                                     T2[:, j, :], ACT.Copy).then_inc(sems["pT_sb"], 1)

                exps(0)
                exps(1)
                copy_pT(0)
                exps(2)
                copy_pT(1)
                exps(3)
                copy_pT(2)
                copy_pT(3)
                for j in range(2):
                    wait("ctx", 2 * j + 2)
                    A.activation(f_hi[:, :, j * 256:(j + 1) * 256].rearrange("p c (a t) -> p a c t", t=P),
                                 Q2[:, j, :].rearrange("p (a c t) -> p a c t", c=KC, t=P), ACT.Copy)\
                        .then_inc(sems["c_hi"], 1)
                wait("var2", 1)
                seed(mv[:, :, 1], nw[:, 0, 0:PAIRS], rs[:, 0, 0:PAIRS], 1.0, 0, "seed3")
                for c in range(KC):
                    wait("x2T", c + 1)
                    A.activation(f_hi[:, c, :], T2[:, c, :], ACT.Copy).then_inc(sems["x2_hi"], 1)
                wait("l_sub", 1)
                A.activation(rt[:, 0], rt[:, 0], ACT.Exp).then_inc(sems["l_exp"], 1)
                wait("cT", 1)
                wait("c_out", 0)
                A.activation(c_sb, S2[0:EXPERTS, 1, :], ACT.Copy).then_inc(sems["c_sb"], 1)

        @block.vector
        def _(dve):
            V = nc.vector
            chain = sems["dve"]
            done = [0]

            def link(ins, base=0):
                done[0] += 1
                ins.then_inc(chain, 1)
                dve.wait_ge(chain, base + done[0])

            def hold():
                dve.sem_inc(s_hold, 1)

            V.memset(eps[:, 0:1], LN_EPS)
            V.memset(eps[:, 1:2], HEAD_EPS).then_inc(s_zero_b, 1)
            V.memset(b_raw[:], 0.0).then_inc(s_zero_b, 1)
            dve.wait_ge(s_zero_y, 1)
            dve.wait_ge(s_w, 16 * 5)
            for t, n in ((w_raw, W_VM), (b_raw, B_V)):
                for a in range(0, n, 512):
                    v = t[:, a:a + 512].rearrange("p (h d) -> p h d", d=HD)
                    link(V.tensor_reduce(mean_w, v, axis=AX, op=ALU.add))
                    link(V.tensor_scalar(mean_w, mean_w, 1.0 / HD, None, ALU.mult))
                    link(V.tensor_tensor(v, v, mean_w.unsqueeze(2).broadcast_to([P, 32, HD]), ALU.subtract))
            V.tensor_copy(mx[:, 1, 0, 0:1], mx[:, 0, 0, 0:1]).then_inc(s_centred, 1)
            dve.wait_ge(s_split_w, 2)
            V.tensor_tensor(w_lo[:], w_raw[:], w_hi[:].bitcast(F32), ALU.subtract).then_inc(s_split_w, 1)
            for r in (32, 96):
                V.tensor_tensor(b_rows[r:r + 1, :], b_raw[r:r + 1, :], b_rows[r:r + 1, :].bitcast(F32), ALU.subtract)\
                    .then_inc(s_split_w, 1)
            before = done[0]
            with dve.Fori(0, GROUPS) as g:
                wait = per_group(dve, g)
                base = g * DVE_LINKS

                def lk(ins):
                    link(ins, base)

                def newton(var, scale, e, y, n):
                    v, t = nw[:, 1, 0:n], nw[:, 2, 0:n]
                    V.tensor_scalar(v, var, scale, e, ALU.mult, ALU.add)
                    lk(V.tensor_tensor(t, y, y, ALU.mult))
                    lk(V.tensor_tensor(t, t, v, ALU.mult))
                    lk(V.tensor_scalar(t, t, -0.5, 1.5, ALU.mult, ALU.add))
                    lk(V.tensor_tensor(y, y, t, ALU.mult))

                def norm(var_name, seed_name, out_name):
                    hold()
                    for p in range(PAIRS):
                        ins = V.bn_stats(st[:, p, :], x1[:, ds(g * PAIRS + p, 1), :].rearrange("p a d -> p (a d)"))
                    lk(ins)
                    hold()
                    for p in range(PAIRS):
                        ins = V.bn_aggr(mv[:, p, :], st[:, p, :])
                    ins.then_inc(sems[var_name], 1)
                    wait(seed_name, 1)
                    wait(var_name, 1)
                    y = rs[:, 0, 0:PAIRS]
                    newton(mv[:, :, 1], 1.0, LN_EPS, y, PAIRS)
                    for p in range(PAIRS):
                        V.tensor_scalar(xn[:, p, :], x1[:, ds(g * PAIRS + p, 1), :].rearrange("p a d -> p (a d)"),
                                        mv[:, p, 0:1], rs[:, 0, p:p + 1], ALU.subtract, ALU.mult)\
                            .then_inc(sems[out_name], 1)

                wait("x_in", 16)
                norm("var1", "seed1", "xn")
                for c in range(KC):
                    wait("x_hi", c + 1)
                    V.tensor_tensor(f_lo[:, c, :], T2[:, c, :], f_hi[:, c, :].bitcast(F32), ALU.subtract)\
                        .then_inc(sems["x_lo"], 1)
                n = PAIRS * HEADS
                for i, (src, dst, sq_name, name) in enumerate(((Q2, qn, "q_sq", "qn"), (K2, kn, "k_sq", "kn"))):
                    for j in range(2):
                        wait(sq_name, j + 1)
                        sq = prob[i][:].rearrange("p h s -> p (h s)")[:, j * 512:(j + 1) * 512]
                        ins = V.tensor_reduce(ss[:, i * n + j * 32:i * n + (j + 1) * 32],
                                              sq.rearrange("p (h d) -> p h d", d=HD), axis=AX, op=ALU.add)
                        if j == 0:
                            lk(ins)
                    ins.then_inc(sems["ssq"], 1)
                for i, (src, dst, sq_name, name) in enumerate(((Q2, qn, "q_sq", "qn"), (K2, kn, "k_sq", "kn"))):
                    wait("ssq", i + 1)
                    wait("seed2", i + 1)
                    newton(ss[:, i * n:(i + 1) * n], 1.0 / HD, HEAD_EPS, rs[:, i, :], n)
                    for j in range(2):
                        V.tensor_tensor(dst[:, 2 * j:2 * j + 2, :].rearrange("p a (h d) -> p (a h) d", d=HD),
                                        src[:, j, :].rearrange("p (h d) -> p h d", d=HD),
                                        rs[:, i, 32 * j:32 * j + 32].unsqueeze(2).broadcast_to([P, 32, HD]), ALU.mult)\
                            .then_inc(sems[name], 1)

                def diagonal_v(p):
                    wait("v", p + 1)
                    if p == 0:
                        wait("ctx", 0)
                    v = Q2[:, p % 2, :].rearrange("p (t h e d) -> p t h e d", t=2, e=2, d=HD)
                    V.tensor_copy(v_diag[0:SEQ, 2 * p:2 * p + 2, :, 0, :], v[0:SEQ, :, :, 0, :])
                    V.tensor_copy(v_diag[SEQ:P, 2 * p, :, 1, :], v[SEQ:P, 1, :, 1, :])
                    V.tensor_copy(v_diag[SEQ:P, 2 * p + 1, :, 1, :], v[SEQ:P, 0, :, 1, :]).then_inc(sems["v_diag"], 1)

                for p in range(PAIRS):
                    diagonal_v(p)
                kinds = ((0, MAIN), (MAIN, SEQ))

                def subtract_max(p):
                    wait("s", p + 1)
                    if p >= 2:
                        wait("pT", 2 * (p - 1))
                    wait("s_sub", max(p - 1, 0))
                    S = (K2, S2)[p % 2][:].rearrange("p c (h s) -> p (c h) s", s=SEQ)
                    for i, (a, b) in enumerate(kinds):
                        ins = V.tensor_reduce(mx[:, p % 2, i, :], S[:, :, a:b], axis=AX, op=ALU.max)
                    lk(ins)
                    for i, (a, b) in enumerate(kinds):
                        ins = V.tensor_tensor(prob[p % 2][:, :, a:b], S[:, :, a:b],
                                              mx[:, p % 2, i, :].unsqueeze(2).broadcast_to([P, HEADS, b - a]), ALU.subtract)
                    ins.then_inc(sems["s_sub"], 1)

                def sums(p):
                    wait("s_exp", p + 1)
                    for i, (a, b) in enumerate(kinds):
                        ins = V.tensor_reduce(sm[:, p % 2, i, :], prob[p % 2][:, :, a:b], axis=AX, op=ALU.add)
                    lk(ins)
                    V.reciprocal(sm[:, p % 2], sm[:, p % 2]).then_inc(sems["s_rcp"], 1)

                subtract_max(0)
                subtract_max(1)
                sums(0)
                subtract_max(2)
                sums(1)
                subtract_max(3)
                sums(2)
                sums(3)
                for j in range(2):
                    wait("c_hi", j + 1)
                    V.tensor_tensor(f_lo[:, :, j * 256:(j + 1) * 256].rearrange("p c (a t) -> p a c t", t=P),
                                    Q2[:, j, :].rearrange("p (a c t) -> p a c t", c=KC, t=P),
                                    f_hi[:, :, j * 256:(j + 1) * 256].bitcast(F32).rearrange("p c (a t) -> p a c t", t=P),
                                    ALU.subtract).then_inc(sems["c_lo"], 1)
                for j in range(2):
                    wait("o", j + 1)
                    t = x1[:, ds(g * PAIRS + 2 * j, 2), :]
                    ins = V.tensor_tensor(t, K2[:, j, :].rearrange("p (a d) -> p a d", d=D), t, ALU.add)
                lk(ins)
                norm("var2", "seed3", "xn2")
                for c in range(KC):
                    wait("x2_hi", c + 1)
                    V.tensor_tensor(f_lo[:, c, :], T2[:, c, :], f_hi[:, c, :].bitcast(F32), ALU.subtract)\
                        .then_inc(sems["x2_lo"], 1)
                wait("logit", 1)
                wait("c_out", 0)
                L = S2[:, 0, 0:PAIRS * EXPERTS].rearrange("p (a e) -> p a e", e=EXPERTS)
                wide = [P, PAIRS, EXPERTS]

                def col(i):
                    return r1[:, i, :].unsqueeze(2).broadcast_to(wide)

                lk(V.tensor_reduce(r1[:, 0, :], L, axis=AX, op=ALU.max))
                V.tensor_tensor(rt[:, 0], L, col(0), ALU.subtract).then_inc(sems["l_sub"], 1)
                wait("l_exp", 1)
                lk(V.tensor_reduce(r1[:, 1, :], rt[:, 0], axis=AX, op=ALU.add))
                lk(V.reciprocal(r1[:, 1, :], r1[:, 1, :]))
                lk(V.tensor_tensor(rt[:, 0], rt[:, 0], col(1), ALU.mult))
                hold()
                for p in range(PAIRS):
                    ins = V.max(r8[:, 0, p, :], rt[:, 0, p, :])
                lk(ins)
                hold()
                for p in range(PAIRS):
                    ins = V.match_replace(rt[:, 1, p, :], r8[:, 0, p, :], rt[:, 0, p, :], -1.0)
                lk(ins)
                lk(V.tensor_scalar(rt[:, 1], rt[:, 1], 0.0, None, ALU.is_lt))
                lk(V.tensor_reduce(r1[:, 2, :], r8[:, 0], axis=AX, op=ALU.add))
                lk(V.tensor_scalar(r1[:, 2, :], r1[:, 2, :], 1e-12, None, ALU.max))
                lk(V.reciprocal(r1[:, 2, :], r1[:, 2, :]))
                lk(V.tensor_tensor(rt[:, 2], rt[:, 0], col(2), ALU.mult))
                lk(V.tensor_tensor(r8[:, 1], r8[:, 0], r1[:, 2, :].unsqueeze(2).broadcast_to([P, PAIRS, TOP_K]), ALU.mult))
                lk(V.tensor_scalar(rt[:, 3], rt[:, 2], par[:, PAR_ALPHA:PAR_ALPHA + 1], None, ALU.mult))
                lk(V.tensor_scalar(r8[:, 1], r8[:, 1], par[:, PAR_ALPHA:PAR_ALPHA + 1], None, ALU.mult))
                lk(V.tensor_reduce(r1[:, 3, :], r8[:, 1], axis=AX, op=ALU.max))
                lk(V.tensor_scalar(rt[:, 4], rt[:, 3], TAU, None, ALU.is_ge))
                lk(V.tensor_scalar(r1[:, 4, :], r1[:, 3, :], TAU, None, ALU.is_lt))
                lk(V.tensor_tensor(rt[:, 5], rt[:, 3], col(3), ALU.is_equal))
                lk(V.tensor_tensor(rt[:, 5], rt[:, 5], rt[:, 1], ALU.mult))
                lk(V.tensor_tensor(rt[:, 6], rt[:, 5], rt[:, 0], ALU.mult))
                lk(V.tensor_reduce(r1[:, 5, :], rt[:, 6], axis=AX, op=ALU.max))
                lk(V.tensor_tensor(rt[:, 6], rt[:, 0], col(5), ALU.is_equal))
                lk(V.tensor_tensor(rt[:, 5], rt[:, 5], rt[:, 6], ALU.mult))
                lk(V.tensor_tensor(rt[:, 5], rt[:, 5],
                                   con[:, C_IOTA:C_IOTA + EXPERTS].unsqueeze(1).broadcast_to(wide), ALU.mult))
                lk(V.tensor_reduce(r1[:, 6, :], rt[:, 5], axis=AX, op=ALU.max))
                lk(V.tensor_tensor(rt[:, 5], con[:, C_IOTA:C_IOTA + EXPERTS].unsqueeze(1).broadcast_to(wide), col(6), ALU.is_equal))
                lk(V.tensor_tensor(rt[:, 5], rt[:, 5], col(4), ALU.mult))
                lk(V.tensor_tensor(rt[:, 4], rt[:, 4], rt[:, 5], ALU.max))
                lk(V.tensor_tensor(rt[:, 4], rt[:, 4], rt[:, 1], ALU.mult))
                lk(V.tensor_tensor(rt[:, 4], rt[:, 4], rt[:, 2], ALU.mult))
                lk(V.tensor_reduce(r1[:, 7, :], rt[:, 4], axis=AX, op=ALU.add))
                lk(V.tensor_scalar(r1[:, 7, :], r1[:, 7, :], 1e-12, None, ALU.max))
                lk(V.reciprocal(r1[:, 7, :], r1[:, 7, :]))
                V.tensor_tensor(rt[:, 7], rt[:, 4], col(7), ALU.mult).then_inc(sems["comb"], 1)
                wait("comb", 1)
            assert done[0] - before == DVE_LINKS, done[0] - before

        @block.tensor
        def _(pe):
            T = nc.tensor
            pe.wait_ge(s_split_w, 7)
            with pe.Fori(0, GROUPS) as g:
                wait = per_group(pe, g)

                def split_product(dst, left, right, first, last):
                    T.matmul(dst, left[0], right[0], start=first, stop=False)
                    T.matmul(dst, left[0], right[1], start=False, stop=False)
                    return T.matmul(dst, left[1], right[0], start=False, stop=last)

                def transposes(name_in, src, name_out):
                    for c in range(KC):
                        for p in range(PAIRS):
                            if c == 0:
                                wait(name_in, p + 1)
                            ins = T.transpose(T2[:, c, p * P:(p + 1) * P], src[:, p, c * P:(c + 1) * P], ident)
                        ins.then_inc(sems[name_out], 1)

                wait("x2_lo", 0)
                transposes("xn", xn, "xT")
                wait("x_lo", 2)
                wait("c_lo", 0)
                for j in range(2):
                    for p in (2 * j, 2 * j + 1):
                        dst = Q2[:, j, (p % 2) * D:(p % 2 + 1) * D]
                        T.matmul(dst, ones_all[:], b_rows[:, B_Q:B_Q + D], start=True, stop=False)
                        for c in range(KC):
                            w = slice(W_Q + c * D, W_Q + (c + 1) * D)
                            ins = split_product(dst, (f_hi[:, c, p * P:(p + 1) * P], f_lo[:, c, p * P:(p + 1) * P]),
                                                (w_hi[:, w], w_lo[:, w]), False, c == KC - 1)
                    ins.then_inc(sems["q"], 1)

                def context(dst, rows, bias, cols):
                    T.matmul(dst, ones_kind[:], b_rows[:, bias:bias + D], start=True, stop=False)
                    for i, w in enumerate(cols):
                        ins = split_product(dst, (rows(y_hi[i][:]), rows(y_lo[i][:])),
                                            (w_hi[:, w:w + D], w_lo[:, w:w + D]), False, i == 1)
                    return ins

                wait("y_lo", 2)
                wait("var2", 0)
                for j in range(2):
                    for p in (2 * j, 2 * j + 1):
                        ins = context(K2[:, j, (p % 2) * D:(p % 2 + 1) * D],
                                      lambda t: t[:, p, 0:2, :].rearrange("p a s -> p (a s)"), B_K, (W_KM, W_KD))
                    ins.then_inc(sems["k"], 1)
                for c in range(KC):
                    for p in range(PAIRS):
                        if c == 0 and p % 2 == 0:
                            wait("qn", p // 2 + 1)
                        ins = T.transpose(T2[:, c, p * P:(p + 1) * P], qn[:, p, c * P:(c + 1) * P], ident)
                    ins.then_inc(sems["qT"], 1)
                wait("c_sb", 0)
                for c in range(KC):
                    for p in range(PAIRS):
                        if c == 0 and p % 2 == 0:
                            wait("kn", p // 2 + 1)
                        ins = T.transpose(S2[:, c, p * P:(p + 1) * P], kn[:, p, c * P:(c + 1) * P], ident)
                    ins.then_inc(sems["kT"], 1)
                for p in range(PAIRS):
                    if p >= 2:
                        wait("v_diag", p - 1)
                    for b in range(2):
                        ins = context(Q2[:, p % 2, b * D:(b + 1) * D],
                                      lambda t: t[:, p, b:b + 2, :].rearrange("p a s -> p (a s)"),
                                      B_V, (W_VM, W_VD))
                    ins.then_inc(sems["v"], 1)

                def scores(p):
                    wait("k_diag", p + 1)
                    if p == 0:
                        wait("qT_sb", 2)
                    if p >= 2:
                        wait("s_sub", p - 1)
                    for c in range(KC):
                        for b in range(2):
                            S = (K2, S2)[p % 2]
                            t = p * P + b * SEQ
                            ins = T.matmul(S[b * SEQ:(b + 1) * SEQ, c, :], qT[:, c, t:t + SEQ],
                                           k_diag[p % 2][:, c, b, :, :].rearrange("p h s -> p (h s)"),
                                           start=True, stop=True)
                    ins.then_inc(sems["s"], 1)

                def attend(p):
                    wait("prob", p + 1)
                    if p >= 1:
                        wait("pT_sb", 2 * p)
                    flat = prob[p % 2][:].rearrange("p h s -> p (h s)")
                    for j in range(2):
                        for i in range(4):
                            h = 4 * j + i
                            ins = T.transpose(T2[:, j, i * P:(i + 1) * P], flat[:, h * P:(h + 1) * P], ident)
                        ins.then_inc(sems["pT"], 1)
                    if p == 0:
                        wait("v_diag", 4)
                    wait("pT_sb", 2 * p + 2)
                    for c in range(KC):
                        for b in range(2):
                            for i in range(4):
                                h = 4 * c + i
                                col = ((p % 2) * KC + c) * P + b * SEQ
                                ins = T.matmul(Q2[32 * i:32 * i + 32, p // 2, col:col + SEQ],
                                               v_diag[:, 2 * p + b, h].rearrange("p e d -> p (e d)"),
                                               pT[p % 2][:, h, b * SEQ:(b + 1) * SEQ], start=True, stop=True)
                    ins.then_inc(sems["ctx"], 1)

                scores(0)
                scores(1)
                attend(0)
                scores(2)
                attend(1)
                scores(3)
                attend(2)
                attend(3)
                wait("s_sub", 4)
                for j in range(2):
                    wait("c_lo", j + 1)
                    for p in (2 * j, 2 * j + 1):
                        dst = K2[:, j, (p % 2) * D:(p % 2 + 1) * D]
                        T.matmul(dst, ones_all[:], b_rows[:, B_O:B_O + D], start=True, stop=False)
                        for c in range(KC):
                            w = slice(W_O + c * D, W_O + (c + 1) * D)
                            ins = split_product(dst, (f_hi[:, c, p * P:(p + 1) * P], f_lo[:, c, p * P:(p + 1) * P]),
                                                (w_hi[:, w], w_lo[:, w]), False, c == KC - 1)
                    ins.then_inc(sems["o"], 1)
                transposes("xn2", xn, "x2T")
                wait("x2_lo", 2)
                for p in range(PAIRS):
                    dst = S2[:, 0, p * EXPERTS:(p + 1) * EXPERTS]
                    for c in range(KC):
                        w = slice(W_G + c * EXPERTS, W_G + (c + 1) * EXPERTS)
                        t = slice(p * P, (p + 1) * P)
                        ins = split_product(dst, (f_hi[:, c, t], f_lo[:, c, t]), (w_hi[:, w], w_lo[:, w]),
                                            c == 0, c == KC - 1)
                ins.then_inc(sems["logit"], 1)
                wait("comb", 1)
                for p in range(PAIRS):
                    ins = T.transpose(S2[0:EXPERTS, 1, p * P:(p + 1) * P], rt[:, 7, p, :], ident)
                ins.then_inc(sems["cT"], 1)

    made = ("gate", "up", "silu", "scaled", "h", "h_hi", "h_lo", "down", "dn_hi", "dn_lo")
    ev = {n: nc.alloc_semaphore(f"e_{n}") for n in made}
    s_cb = [nc.alloc_semaphore(f"e_cb{i}") for i in range(SLOTS)]
    s_dn = [nc.alloc_semaphore(f"e_dn{i}") for i in range(SLOTS)]
    s_split, s_split_lo, s_acc_sb, s_yT, s_y, s_out = (nc.alloc_semaphore(f"e_{n}") for n in
                                                      ("split", "split_lo", "acc_sb", "yT", "y", "out"))
    G8 = [ps[0][:, 0, :], ps[0][:, 1, :]]
    U8 = [ps[1][:, 0, :], ps[1][:, 1, :]]
    ACC, YT = ps[2], ps[3]

    def waits(engine):
        def wait(name, g, j, back=0):
            engine.wait_ge(ev[name], g * CHUNKS + j + (1 + CREDIT - back))
        return wait

    with nc.Block() as block2:

        @block2.sync
        def _(sp):
            for sem in (s_acc_sb, s_yT, s_y, s_out):
                sp.sem_inc(sem, 1)
            with sp.Fori(0, GROUPS) as g:
                def triple(m, wait_free):
                    for r in range(SLOTS):
                        c = g * CHUNKS + m * SLOTS + r
                        if wait_free:
                            sp.wait_ge(ev["scaled"], c + (1 + CREDIT - SLOTS))
                        cut = (96, 64, 32)[r]
                        for e, a, b in ((r, 0, cut), (r + 1, cut, P)):
                            src = c_dram[ds(m * 4 + e, 1), ds(g * GROUP, GROUP)].broadcast_to([b - a, GROUP])
                            sp.dma_start(cb[r][a:b, :], src).then_inc(s_cb[r], 16)
                        sp.wait_ge(ev["dn_lo"], c + (1 + CREDIT - SLOTS))
                        sp.dma_start(dn_raw[r][:], w_down[ds(m * SLOTS + r, 1), :, :].rearrange("a p d -> (a p) d"))\
                            .then_inc(s_dn[r], 16)
                with sp.Fori(0, CHUNKS // SLOTS) as m:
                    triple(m, True)
                sp.wait_ge(s_y, g * 2 + 3)
                sp.dma_start(out[:, ds(g * PAIRS, PAIRS), :], y_out[:]).then_inc(s_out, 16)
            sp.wait_ge(s_out, 16 * GROUPS + 1)

        def run(engine, body, after_group):
            with engine.Fori(0, GROUPS) as g:
                for j in range(CHUNKS):
                    body(g, j, g * (CHUNKS // SLOTS) + (j // SLOTS + 1))
                if after_group:
                    after_group(g)

        @block2.gpsimd
        def _(pool):
            G = nc.gpsimd
            wait = waits(pool)
            for name in ("scaled", "dn_lo"):
                pool.sem_inc(ev[name], CREDIT)

            def body(g, j, fills):
                r = j % SLOTS
                wait("silu", g, j)
                pool.wait_ge(s_cb[r], fills * 32)
                G.tensor_tensor(hid[r][:], hid[r][:], cb[r][:], ALU.mult).then_inc(ev["scaled"], 1)
                wait("dn_hi", g, j)
                wait("down", g, j, SLOTS)
                G.tensor_tensor(dn_lo[r][:], dn_raw[r][:], dn_hi[r][:].bitcast(F32), ALU.subtract)\
                    .then_inc(ev["dn_lo"], 1)

            run(pool, body, None)

        @block2.scalar
        def _(act):
            A = nc.scalar
            wait = waits(act)
            for name in ("silu", "h_hi", "dn_hi"):
                act.sem_inc(ev[name], CREDIT)
            act.wait_ge(s_raw, 64)
            for j in range(0, CHUNKS, 2):
                A.activation(up_hi[:, j:j + 2].rearrange("p a k g f -> p (a k g f)"),
                             up_raw[:, j:j + 2].rearrange("p a k g f -> p (a k g f)"), ACT.Copy).then_inc(s_split, 1)

            def body(g, j, fills):
                r = j % SLOTS
                wait("down", g, j, SLOTS)
                act.wait_ge(s_dn[r], fills * 16)
                A.activation(dn_hi[r][:], dn_raw[r][:], ACT.Copy).then_inc(ev["dn_hi"], 1)
                wait("gate", g, j)
                wait("h_lo", g, j, SLOTS)
                A.activation(hid[r][:], G8[j % 2], ACT.Silu).then_inc(ev["silu"], 1)
                wait("h", g, j)
                wait("down", g, j, 2)
                A.activation(h_hi[j % 2][:], hid[r][:], ACT.Copy).then_inc(ev["h_hi"], 1)

            def after(g):
                wait("down", g, CHUNKS - 1)
                act.wait_ge(s_yT, g * 2 + 1)
                A.activation(acc_sb[:, 0, :], ACC[:, 0, :], ACT.Copy).then_inc(s_acc_sb, 1)

            run(act, body, after)

        @block2.vector
        def _(dve):
            V = nc.vector
            wait = waits(dve)
            for name in ("h", "h_lo"):
                dve.sem_inc(ev[name], CREDIT)
            for j in range(0, CHUNKS, 2):
                dve.wait_ge(s_split, j // 2 + 1)
                V.tensor_tensor(up_lo[:, j:j + 2].rearrange("p a k g f -> p (a k g f)"),
                                up_raw[:, j:j + 2].rearrange("p a k g f -> p (a k g f)"),
                                up_hi[:, j:j + 2].bitcast(F32).rearrange("p a k g f -> p (a k g f)"),
                                ALU.subtract).then_inc(s_split_lo, 1)

            def body(g, j, fills):
                r = j % SLOTS
                wait("scaled", g, j)
                wait("up", g, j)
                V.tensor_tensor(hid[r][:], U8[j % 2], hid[r][:], ALU.mult).then_inc(ev["h"], 1)
                wait("h", g, j)
                wait("h_hi", g, j)
                wait("down", g, j, 2)
                V.tensor_tensor(h_lo[j % 2][:], hid[r][:], h_hi[j % 2][:].bitcast(F32), ALU.subtract)\
                    .then_inc(ev["h_lo"], 1)

            def after(g):
                wait("down", g, CHUNKS - 1)
                dve.wait_ge(s_yT, g * 2 + 1)
                V.tensor_copy(acc_sb[:, 1, :], ACC[:, 1, :]).then_inc(s_acc_sb, 1)
                dve.wait_ge(s_out, g * 16 + 1)
                for i in range(2):
                    dve.wait_ge(s_yT, g * 2 + i + 2)
                    V.tensor_tensor(y_out[:, 2 * i:2 * i + 2, :], YT[:, i, :].rearrange("p (a d) -> p a d", d=D),
                                    x1[:, ds(g * PAIRS + 2 * i, 2), :], ALU.add).then_inc(s_y, 1)

            run(dve, body, after)

        @block2.tensor
        def _(pe):
            T = nc.tensor
            wait = waits(pe)
            for name in ("gate", "up", "down"):
                pe.sem_inc(ev[name], CREDIT)
            pe.wait_ge(s_split_lo, CHUNKS // 2)

            def up(g, j):
                for i, (dst, name, free) in enumerate(((G8[j % 2], "gate", "silu"), (U8[j % 2], "up", "h"))):
                    wait(free, g, j, 2)
                    for c in range(KC):
                        t = ds(g * GROUP, GROUP)
                        hi, lo = up_hi[:, j, c, i, :], up_lo[:, j, c, i, :]
                        T.matmul(dst, hi, x2_hi[:, c, t], start=c == 0, stop=False)
                        T.matmul(dst, hi, x2_lo[:, c, t], start=False, stop=False)
                        ins = T.matmul(dst, lo, x2_hi[:, c, t], start=False, stop=c == KC - 1)
                    ins.then_inc(ev[name], 1)

            def down(g, j):
                first, last = j == 0, j == CHUNKS - 1
                wait("h_lo", g, j)
                wait("dn_lo", g, j)
                r = j % SLOTS
                if first:
                    pe.wait_ge(s_acc_sb, g * 2 + 1)
                for m in range(KC):
                    f = slice(m * P, (m + 1) * P)
                    T.matmul(ACC[:, m, :], dn_hi[r][:, f], h_hi[j % 2][:], start=first, stop=False)
                    T.matmul(ACC[:, m, :], dn_hi[r][:, f], h_lo[j % 2][:], start=False, stop=False)
                    ins = T.matmul(ACC[:, m, :], dn_lo[r][:, f], h_hi[j % 2][:], start=False, stop=last)
                ins.then_inc(ev["down"], 1)

            def body(g, j, fills):
                up(g, j)
                if j >= LAG:
                    down(g, j - LAG)

            def after(g):
                for j in range(CHUNKS - LAG, CHUNKS):
                    down(g, j)
                pe.wait_ge(s_acc_sb, g * 2 + 3)
                pe.wait_ge(s_y, g * 2 + 1)
                for p in range(PAIRS):
                    for m in range(KC):
                        ins = T.transpose(YT[:, p // 2, ((p % 2) * KC + m) * P:((p % 2) * KC + m + 1) * P],
                                          acc_sb[:, m, p * P:(p + 1) * P], ident)
                    if p % 2:
                        ins.then_inc(s_yT, 1)

            run(pe, body, after)


def kernel(**inputs):
    import concourse.bacc as bacc
    from concourse.bass_utils import run_bass_kernel_spmd

    a = {k.replace("L0_xattn_", "").replace("L0_ffn_", ""): np.asarray(v) for k, v in inputs.items()}

    def rows(t, n):
        return t.reshape(n, P, -1).transpose(1, 0, 2).reshape(P, -1)

    kv = np.concatenate([a["Wk"], a["Wv"]], axis=1).reshape(CTX, HEADS, 2, HD)
    b_kv = np.concatenate([a["bk"], a["bv"]]).reshape(HEADS, 2, HD)
    w_attn = np.concatenate([
        rows(a["Wq"], KC), kv[:, :, 0].reshape(CTX, D), a["Wkv_dca"][:, :D],
        kv[:, :, 1].reshape(CTX, D), a["Wkv_dca"][:, D:], rows(a["Wo"], KC), rows(a["gate_weight"].T, KC)], axis=1)
    b_attn = np.zeros((2, 4 * D), np.float32)
    b_attn[0] = np.concatenate([a["bq"], b_kv[:, 0].ravel(), b_kv[:, 1].ravel(), a["bo"]])
    b_attn[1, D:3 * D] = a["bkv_dca"]
    consts = np.zeros((P, C_END), np.float32)
    consts[:, C_ID:C_ID + P] = np.eye(P)
    for p in range(P):
        consts[p, C_KMASK + p // HD] = 1
    consts[[0, 32], C_ALL:C_ALL + P] = 1
    for b in range(2):
        consts[[0, 32], C_KIND + b * SEQ:C_KIND + b * SEQ + MAIN] = 1
        consts[[64, 96], C_KIND + b * SEQ + MAIN:C_KIND + (b + 1) * SEQ] = 1
    consts[:, C_IOTA:C_IOTA + EXPERTS] = EXPERTS - np.arange(EXPERTS)
    params = np.zeros((P, PAR_END), np.float32)
    for i, n in enumerate(("qn_w", "qn_b", "kn_w", "kn_b", "kn_dca_w", "kn_dca_b")):
        params[:, i] = np.tile(a[n], HC)
    params[:, PAR_ALPHA] = a["layer_alpha"]
    gu = a["gate_up_proj"].reshape(EXPERTS, 2, INTER, D).transpose(1, 0, 2, 3).reshape(2, CHUNKS, P, KC, P)
    arrays = dict(
        x=a["x"].reshape(TOKENS, D), yT=a["ctx_1024"].reshape(TOKENS, CTX).T, w_attn=w_attn, b_attn=b_attn,
        consts=consts, params=params,
        w_up=gu.transpose(4, 1, 3, 0, 2),
        w_down=a["down_proj"].transpose(0, 2, 1).reshape(CHUNKS, P, D),
    )
    arrays = {n: np.ascontiguousarray(t) for n, t in arrays.items()}
    nc = bacc.Bacc("TRN2", target_bir_lowering=False, num_devices=1)
    aps = {n: nc.dram_tensor(n, t.shape, F32, kind="ExternalInput").ap() for n, t in arrays.items()}
    out = nc.dram_tensor("out", (TOKENS, D), F32, kind="ExternalOutput").ap()
    c_dram = nc.dram_tensor("c_dram", (EXPERTS, TOKENS), F32, kind="Internal").ap()
    aps["x"] = aps["x"].rearrange("(a p) d -> p a d", p=P)
    build(nc, **aps, out=out.rearrange("(a p) d -> p a d", p=P), c_dram=c_dram)
    r = run_bass_kernel_spmd(nc, [arrays], core_ids=[0])
    return r.results[0]["out"].reshape(BATCH, SEQ, D)
```

```python
import numpy as np

import concourse.bass as bass
from concourse import mybir
from concourse.bass import ds

F32 = mybir.dt.float32
F32R = mybir.dt.float32r
ALU = mybir.AluOpType
ACT = mybir.ActivationFunctionType
AX = mybir.AxisListType.X

P = 128
BATCH, SEQ, D = 32, 64, 256
TOKENS = BATCH * SEQ
CTX, DCA = 128, 16
MAIN = SEQ - DCA
HEADS, HD = 16, 16
HC = HEADS // 2
RT = 4
EXPERTS, INTER, TOP_K = 32, 96, 8
TAU = 0.05
LN_EPS, HEAD_EPS = 1e-5, 1e-6
GROUP = 512
GROUPS = TOKENS // GROUP
PAIRS = GROUP // P
KC = D // P
CHUNKS = EXPERTS * INTER // P
SLOTS = 3
CREDIT = 3
LAG = 2

W_Q, W_KM, W_KD, W_VM, W_VD, W_O, W_G, W_END = 0, 512, 768, 1024, 1280, 1536, 2048, 2112
B_Q, B_K, B_V, B_O = 0, 256, 512, 768
C_ID, C_ODD, C_ALL, C_KIND, C_END = 0, 128, 130, 258, 386
PAR_QW, PAR_QB, PAR_K, PAR_ALPHA, PAR_END = 0, 1, 2, 6, 7


def build(nc, x, yT, w_attn, b_attn, consts, params, w_up, w_down, out, c_dram):
    place = [nc.sbuf_base + (-nc.sbuf_base) % 64]
    top = nc.sbuf_usable_end

    def at(cursor, name, shape, dt=F32):
        size = int(np.prod(shape[1:])) * 4
        t = nc.alloc_sbuf_tensor_at(name, shape, dt, offset=cursor[0])
        cursor[0] += size + (-size) % 32
        assert cursor[0] <= top, (name, cursor[0], top)
        return t

    x2_hi = at(place, "x2_hi", [P, KC, TOKENS], F32R)
    x2_lo = at(place, "x2_lo", [P, KC, TOKENS], F32R)
    x1 = at(place, "x1", [P, GROUPS * PAIRS, D])
    lo_at = [place[0]]
    up_raw = at(place, "up_raw", [P, CHUNKS, KC, 2, P])
    up_lo = at(lo_at, "up_lo", [P, CHUNKS, KC, 2, P], F32R)
    con = at(place, "con", [P, C_END])
    ident = con[:, C_ID:C_ID + P]

    a1 = [place[0]]
    w_hi = at(a1, "w_hi", [P, W_END], F32R)
    w_lo = at(a1, "w_lo", [P, W_END], F32R)
    b_rows = at(a1, "b_rows", [P, 4 * D], F32R)
    ones_all = at(a1, "ones_all", [P, P], F32R)
    ones_kind = at(a1, "ones_kind", [P, P], F32R)
    par = at(a1, "par", [P, PAR_END])
    y_raw = at(a1, "y_raw", [P, TOKENS])
    y_hi = [at(a1, f"y_hi{i}", [P, PAIRS, 3, SEQ], F32R) for i in range(2)]
    y_lo = [at(a1, f"y_lo{i}", [P, PAIRS, 3, SEQ], F32R) for i in range(2)]
    f_hi = at(a1, "f_hi", [P, KC, GROUP], F32R)
    f_lo = at(a1, "f_lo", [P, KC, GROUP], F32R)
    xn = at(a1, "xn", [P, PAIRS, D])
    raw_at = [a1[0]]
    qn = at(a1, "qn", [P, PAIRS, D])
    kn = at(a1, "kn", [P, PAIRS, D])
    sq = [at(a1, f"sq{i}", [P, 512]) for i in range(2)]
    qT = at(a1, "qT", [P, KC, GROUP])
    k_diag = at(a1, "k_diag", [P, KC, 2 * PAIRS, 2, SEQ])
    w_raw = at(raw_at, "w_raw", [P, W_END])
    b_raw = at(raw_at, "b_raw", [P, 4 * D])
    assert raw_at[0] <= a1[0]
    v_diag = at(a1, "v_diag", [P, 2 * PAIRS, HC, 2, HD])
    prob = [at(a1, f"prob{i}", [P, HEADS, SEQ]) for i in range(2)]
    pT = [at(a1, f"pT{i}", [P, HC, P]) for i in range(2)]
    eps = at(a1, "eps", [P, 2])
    par_k = at(a1, "par_k", [P, 2, 4])
    st = at(a1, "st", [P, PAIRS, 6])
    mv = at(a1, "mv", [P, 2, PAIRS, 2])
    ln = at(a1, "ln", [P, 2, PAIRS])
    rl = at(a1, "rl", [P, 2, PAIRS])
    ss = at(a1, "ss", [P, 2, PAIRS * HEADS])
    rs = at(a1, "rs", [P, 2, PAIRS * HEADS])
    nw = at(a1, "nw", [P, 3, PAIRS * HEADS])
    mx = at(a1, "mx", [P, 2, 2, HEADS])
    sm = at(a1, "sm", [P, 2, 2, HEADS])
    mean_w = mx[:, 0].rearrange("p a b -> p (a b)")
    rt = at(a1, "rt", [P, 5, PAIRS, EXPERTS])
    r8 = at(a1, "r8", [P, 5, PAIRS, TOP_K])
    r1 = at(a1, "r1", [P, 5, PAIRS])
    combined = at(a1, "combined", [P, PAIRS, EXPERTS])
    c_sb = rt[0:EXPERTS, 0:4, :, :].rearrange("p a b c -> p (a b c)")

    a2 = [place[0]]
    up_hi = at(a2, "up_hi", [P, CHUNKS, KC, 2, P], F32R)
    hid = [at(a2, f"hid{i}", [P, GROUP]) for i in range(SLOTS)]
    h_hi = [at(a2, f"h_hi{i}", [P, GROUP], F32R) for i in range(2)]
    h_lo = [at(a2, f"h_lo{i}", [P, GROUP], F32R) for i in range(2)]
    cb = [at(a2, f"cb{i}", [P, GROUP]) for i in range(SLOTS)]
    dn_raw = [at(a2, f"dn_raw{i}", [P, D]) for i in range(SLOTS)]
    dn_hi = [at(a2, f"dn_hi{i}", [P, D], F32R) for i in range(SLOTS)]
    dn_lo = [at(a2, f"dn_lo{i}", [P, D], F32R) for i in range(SLOTS)]
    acc_sb = at(a2, "acc_sb", [P, KC, GROUP])
    y_out = at(a2, "y_out", [P, PAIRS, D])

    F2 = nc.alloc_psum_tensor("F2", [P, 2, 512], F32)
    M2 = nc.alloc_psum_tensor("M2", [P, 2, 512], F32)
    S4 = nc.alloc_psum_tensor("S4", [P, 4, 512], F32)

    PER = dict(
        x_in=16, var1=1, seed1=1, xn=4, xT=2, x_hi=2, x_lo=2, y_hi=2, y_lo=2, q=2, k=2,
        q_sq=2, k_sq=2, ssq=4, seed2=2, qn=2, kn=2, qT=2, kT=2, qT_sb=2, k_diag=2, v=4, v_diag=4,
        s=4, s_sub=4, s_exp=4, s_rcp=4, prob=4, pT=8, pT_sb=8, ctx=4, c_hi=2, c_lo=2, o=2, var2=1,
        seed3=1, xn2=4, x2T=2, x2_hi=2, x2_lo=2, logit=1, l_sub=1, l_exp=1, comb=1, cT=1, c_sb=1, c_out=16, keep=32,
        dve=0,
    )
    sems = {n: nc.alloc_semaphore(f"s_{n}") for n in PER}
    s_const, s_w, s_centred, s_split_w, s_zero_y, s_zero_b, s_raw, s_ln, s_hold = (
        nc.alloc_semaphore(n) for n in
        ("s_const", "s_w", "s_centred", "s_split_w", "s_zero_y", "s_zero_b", "s_raw", "s_ln", "s_hold"))
    DVE_LINKS = 45
    LN_PER = 4

    AHEAD = dict(v=1, s=1, s_sub=1, ctx=1, x2_lo=1, c_sb=1, c_out=1, v_diag=1, prob=1, x2T=1 + 2, keep=1 + 32)

    def per_group(engine, g):
        def wait(name, n):
            assert n > 0 or n + AHEAD[name] > 0
            engine.wait_ge(sems[name], g * PER[name] + n + AHEAD.get(name, 0))
        return wait

    def splits(hi, lo):
        return ((hi, 0), (hi, 1), (lo, 0))

    with nc.Block() as block:

        @block.sync
        def _(sp):
            for name, n in AHEAD.items():
                sp.sem_inc(sems[name], n)
            sp.dma_start(con[:], consts).then_inc(s_const, 16)
            sp.dma_start(par[:], params).then_inc(s_const, 16)
            sp.dma_start(x1[:, 0:PAIRS, :], x[:, 0:PAIRS, :]).then_inc(sems["x_in"], 16)
            sp.dma_start(y_raw[:], yT).then_inc(s_const, 16)
            for g in range(1, GROUPS):
                sp.wait_ge(sems["x_in"], 16 * g)
                sp.dma_start(x1[:, g * PAIRS:(g + 1) * PAIRS, :], x[:, g * PAIRS:(g + 1) * PAIRS, :])\
                    .then_inc(sems["x_in"], 16)
            for i in range(4):
                n = CHUNKS // 4
                sp.dma_start(up_raw[:, i * n:(i + 1) * n], w_up[:, i * n:(i + 1) * n]).then_inc(s_raw, 16)
            with sp.Fori(0, GROUPS) as g:
                wait = per_group(sp, g)
                wait("x2_lo", 2)
                for keep, part in ((x2_hi, f_hi), (x2_lo, f_lo)):
                    sp.dma_start(keep[:].bitcast(F32)[:, :, ds(g * GROUP, GROUP)], part[:].bitcast(F32)).then_inc(sems["keep"], 16)
                wait("c_sb", 1)
                sp.dma_start(c_dram[:, ds(g * GROUP, GROUP)], c_sb).then_inc(sems["c_out"], 16)
            sp.wait_ge(sems["c_out"], 16 * GROUPS + AHEAD["c_out"])
            sp.wait_ge(sems["keep"], 32 * GROUPS + AHEAD["keep"])

        def pipeline(engine, steps, *chains):
            for step, is_front in steps:
                if is_front:
                    step(0)
            before = [c.n for c in chains]
            with engine.Fori(0, GROUPS - 1) as g:
                for c in chains:
                    c.base = g * c.per_round
                for step, is_front in steps:
                    step(g + 1 if is_front else g)
                for c, n in zip(chains, before):
                    assert c.n - n == c.per_round, (c.n - n)
            for c, n in zip(chains, before):
                c.base, c.n = 0, n + (GROUPS - 1) * c.per_round
            for step, is_front in steps:
                if not is_front:
                    step(GROUPS - 1)

        class Chain:
            def __init__(self, engine, sem, per_round):
                self.engine, self.sem, self.per_round, self.n, self.base = engine, sem, per_round, 0, 0

            def mark(self, ins):
                self.n += 1
                ins.then_inc(self.sem, 1)
                return self.n

            def need(self, n):
                self.engine.wait_ge(self.sem, self.base + n)

            def link(self, ins):
                self.need(self.mark(ins))

        kinds = ((0, MAIN), (MAIN, SEQ))

        @block.gpsimd
        def _(pool):
            G = nc.gpsimd
            G.memset(v_diag[:], 0.0)
            for t in (*y_hi, *y_lo):
                last = G.memset(t[:].bitcast(F32), 0.0)
            last.then_inc(s_zero_y, 1)
            pool.wait_ge(s_zero_y, 1)
            pool.wait_ge(s_const, 48)

            def context_low(g):
                wait = per_group(pool, g)
                y = y_raw[:, ds(g * GROUP, GROUP)].rearrange("p (a b s) -> p a b s", b=2, s=SEQ)
                for i, (a, b) in enumerate(kinds):
                    wait("y_hi", i + 1)
                    for t, n in ((0, 2), (2, 1)):
                        ins = G.tensor_tensor(y_lo[i][:, :, t:t + n, a:b], y[:, :, 0:n, a:b],
                                              y_hi[i][:, :, t:t + n, a:b].bitcast(F32), ALU.subtract)
                    ins.then_inc(sems["y_lo"], 1)

            def normalise(p):
                def step(g):
                    wait = per_group(pool, g)
                    wait("s_rcp", p + 1)
                    for i, (a, b) in enumerate(kinds):
                        t = prob[p % 2][:, :, a:b]
                        ins = G.tensor_tensor(t, t, sm[:, p % 2, i, :].unsqueeze(2).broadcast_to([P, HEADS, b - a]),
                                              ALU.mult)
                    ins.then_inc(sems["prob"], 1)
                return step

            pipeline(pool, [(context_low, True)] + [(normalise(p), False) for p in range(PAIRS)])

        @block.scalar
        def _(act):
            A = nc.scalar
            act.dma_start(w_raw[:], w_attn).then_inc(s_w, 16)
            act.wait_ge(s_zero_b, 2)
            for r in range(4):
                act.dma_start(b_raw[32 * r:32 * r + 1, :], b_attn[r // 2:r // 2 + 1, :]).then_inc(s_w, 16)
            A.preload_act_table_set("natural_log_exp_and_others")
            act.wait_ge(s_centred, 1)
            A.activation(w_hi[:], w_raw[:], ACT.Copy).then_inc(s_split_w, 1)
            A.activation(b_rows[:], b_raw[:], ACT.Copy).then_inc(s_split_w, 1)
            act.wait_ge(s_const, 48)
            A.activation(ones_all[:], con[:, C_ALL:C_ALL + P], ACT.Copy).then_inc(s_split_w, 1)
            A.activation(ones_kind[:], con[:, C_KIND:C_KIND + P], ACT.Copy).then_inc(s_split_w, 1)
            act.wait_ge(s_zero_y, 1)
            lns = Chain(act, s_ln, 4)

            def seed(src, tmp, dst, scale, eps_col, name):
                lns.link(A.activation(tmp, src, ACT.Ln, scale=scale, bias=eps[:, eps_col:eps_col + 1]))
                A.activation(dst, tmp, ACT.Exp, scale=-0.5).then_inc(sems[name], 1)

            def context_high(g):
                wait = per_group(act, g)
                y = y_raw[:, ds(g * GROUP, GROUP)].rearrange("p (a b s) -> p a b s", b=2, s=SEQ)
                wait("v", 0)
                for i, (a, b) in enumerate(kinds):
                    for t, n in ((0, 2), (2, 1)):
                        ins = A.activation(y_hi[i][:, :, t:t + n, a:b], y[:, :, 0:n, a:b], ACT.Copy)
                    ins.then_inc(sems["y_hi"], 1)

            def seed1(g):
                wait = per_group(act, g)
                wait("var1", 1)
                seed(mv[:, 0, :, 1], ln[:, 0, :], rl[:, 0, :], 1.0, 0, "seed1")

            def x_high(g):
                wait = per_group(act, g)
                wait("keep", -32)
                for c in range(KC):
                    wait("xT", c + 1)
                    A.activation(f_hi[:, c, :], F2[:, c, :], ACT.Copy).then_inc(sems["x_hi"], 1)

            def squares(i):
                def step(g):
                    wait = per_group(act, g)
                    name = "qk"[i]
                    for j in range(2):
                        wait(name, j + 1)
                        if i:
                            wait("ssq", j + 1)
                        A.activation(sq[j][:], F2[:, j, :], ACT.Square).then_inc(sems[name + "_sq"], 1)
                return step

            def seed2(i):
                def step(g):
                    wait = per_group(act, g)
                    wait("ssq", 2 * i + 2)
                    seed(ss[:, i, :], nw[:, 0, :], rs[:, i, :], 1.0 / HD, 1, "seed2")
                return step

            def queries(g):
                wait = per_group(act, g)
                wait("s", 0)
                for c in range(KC):
                    wait("qT", c + 1)
                    A.activation(qT[:, c, :], F2[:, c, :], ACT.Identity, scale=par[:, PAR_QW:PAR_QW + 1],
                                 bias=par[:, PAR_QB:PAR_QB + 1]).then_inc(sems["qT_sb"], 1)

            def keys(g):
                wait = per_group(act, g)
                for c in range(KC):
                    wait("kT", c + 1)
                    for i, (a, b) in enumerate(kinds):
                        src = F2[:, c, :].rearrange("p (b s) -> p b s", s=SEQ)[:, :, a:b]
                        for e in range(2):
                            ins = A.activation(k_diag[:, c, :, e, a:b], src, ACT.Identity,
                                               scale=par_k[:, e, 2 * i:2 * i + 1], bias=par_k[:, e, 2 * i + 1:2 * i + 2])
                    ins.then_inc(sems["k_diag"], 1)

            def exps(p):
                def step(g):
                    wait = per_group(act, g)
                    wait("s_sub", p + 1)
                    t = prob[p % 2][:].rearrange("p h s -> p (h s)")
                    A.activation(t, t, ACT.Exp, scale=HD ** -0.5).then_inc(sems["s_exp"], 1)
                return step

            def copy_pT(p, j):
                def step(g):
                    wait = per_group(act, g)
                    wait("ctx", max(p - 1, 0))
                    wait("pT", 2 * p + j + 1)
                    A.activation(pT[p % 2][:, 4 * j:4 * j + 4, :].rearrange("p a b -> p (a b)"),
                                 M2[:, 0, :], ACT.Copy).then_inc(sems["pT_sb"], 1)
                return step

            def ctx_high(j):
                def step(g):
                    wait = per_group(act, g)
                    wait("ctx", 2 * j + 2)
                    wait("keep", 0)
                    A.activation(f_hi[:, :, j * 256:(j + 1) * 256].rearrange("p c (a t) -> p a c t", t=P),
                                 M2[:, 1, :].rearrange("p (a c t) -> p a c t", c=KC, t=P), ACT.Copy)\
                        .then_inc(sems["c_hi"], 1)
                return step

            def seed3(g):
                wait = per_group(act, g)
                wait("var2", 1)
                seed(mv[:, 1, :, 1], ln[:, 1, :], rl[:, 1, :], 1.0, 0, "seed3")

            def x2_high(g):
                wait = per_group(act, g)
                for c in range(KC):
                    wait("x2T", c + 1)
                    A.activation(f_hi[:, c, :], S4[:, 2 + c, :], ACT.Copy).then_inc(sems["x2_hi"], 1)

            def logit_exp(g):
                wait = per_group(act, g)
                wait("l_sub", 1)
                A.activation(rt[:, 0], rt[:, 0], ACT.Exp).then_inc(sems["l_exp"], 1)

            def combine(g):
                wait = per_group(act, g)
                wait("cT", 1)
                wait("c_out", 0)
                A.activation(c_sb, M2[0:EXPERTS, 1, :], ACT.Copy).then_inc(sems["c_sb"], 1)

            pipeline(act, [
                (exps(0), False), (context_high, True), (seed1, True), (x_high, True), (copy_pT(0, 0), False),
                (exps(1), False), (copy_pT(0, 1), False), (squares(0), True), (exps(2), False), (seed2(0), True),
                (copy_pT(1, 0), False), (copy_pT(1, 1), False), (ctx_high(0), False), (copy_pT(2, 0), False),
                (queries, True), (exps(3), False), (copy_pT(2, 1), False), (squares(1), True),
                (copy_pT(3, 0), False), (seed2(1), True), (copy_pT(3, 1), False), (ctx_high(1), False),
                (keys, True), (seed3, False), (x2_high, False), (logit_exp, False), (combine, False)], lns)

        @block.vector
        def _(dve):
            V = nc.vector
            chain = Chain(dve, sems["dve"], DVE_LINKS)
            lk = chain.link

            def hold():
                dve.sem_inc(s_hold, 1)

            V.memset(r8[:, 4], -3.0)
            V.memset(eps[:, 0:1], LN_EPS)
            V.memset(eps[:, 1:2], HEAD_EPS).then_inc(s_zero_b, 1)
            V.memset(b_raw[:], 0.0).then_inc(s_zero_b, 1)
            dve.wait_ge(s_w, 16 * 5)
            for t, n in ((w_raw, W_VM), (b_raw, B_V)):
                for a in range(0, n, 512):
                    v = t[:, a:a + 512].rearrange("p (h d) -> p h d", d=HD)
                    lk(V.tensor_reduce(mean_w, v, axis=AX, op=ALU.add))
                    lk(V.tensor_scalar(mean_w, mean_w, 1.0 / HD, None, ALU.mult))
                    lk(V.tensor_tensor(v, v, mean_w.unsqueeze(2).broadcast_to([P, 32, HD]), ALU.subtract))
            dve.wait_ge(s_const, 48)
            for e in range(2):
                ins = V.tensor_scalar(par_k[:, e, :], par[:, PAR_K:PAR_K + 4], con[:, C_ODD + e:C_ODD + e + 1], None,
                                      ALU.mult)
            ins.then_inc(s_centred, 1)
            dve.wait_ge(s_zero_y, 1)
            dve.wait_ge(s_split_w, 2)
            V.tensor_tensor(w_lo[:], w_raw[:], w_hi[:].bitcast(F32), ALU.subtract).then_inc(s_split_w, 1)
            for r in (32, 96):
                V.tensor_tensor(b_rows[r:r + 1, :], b_raw[r:r + 1, :], b_rows[r:r + 1, :].bitcast(F32), ALU.subtract)\
                    .then_inc(s_split_w, 1)

            def newton(var, scale, e, y, n):
                v, t = nw[:, 1, 0:n], nw[:, 2, 0:n]
                V.tensor_scalar(v, var, scale, e, ALU.mult, ALU.add)
                lk(V.tensor_tensor(t, y, y, ALU.mult))
                lk(V.tensor_tensor(t, t, v, ALU.mult))
                lk(V.tensor_scalar(t, t, -0.5, 1.5, ALU.mult, ALU.add))
                lk(V.tensor_tensor(y, y, t, ALU.mult))

            def moments(g, i, name):
                hold()
                for p in range(PAIRS):
                    ins = V.bn_stats(st[:, p, :], x1[:, ds(g * PAIRS + p, 1), :].rearrange("p a d -> p (a d)"))
                lk(ins)
                hold()
                for p in range(PAIRS):
                    ins = V.bn_aggr(mv[:, i, p, :], st[:, p, :])
                ins.then_inc(sems[name], 1)

            def apply_norm(g, i, wait, var_name, seed_name, out_name):
                wait(seed_name, 1)
                wait(var_name, 1)
                newton(mv[:, i, :, 1], 1.0, LN_EPS, rl[:, i, :], PAIRS)
                for p in range(PAIRS):
                    V.tensor_scalar(xn[:, p, :], x1[:, ds(g * PAIRS + p, 1), :].rearrange("p a d -> p (a d)"),
                                    mv[:, i, p, 0:1], rl[:, i, p:p + 1], ALU.subtract, ALU.mult)\
                        .then_inc(sems[out_name], 1)

            def norm1(g):
                wait = per_group(dve, g)
                wait("x_in", 16)
                wait("x2T", -2)
                moments(g, 0, "var1")

            def norm1_apply(g):
                apply_norm(g, 0, per_group(dve, g), "var1", "seed1", "xn")

            def x_low(g):
                wait = per_group(dve, g)
                for c in range(KC):
                    wait("x_hi", c + 1)
                    V.tensor_tensor(f_lo[:, c, :], F2[:, c, :], f_hi[:, c, :].bitcast(F32), ALU.subtract)\
                        .then_inc(sems["x_lo"], 1)

            def square_sums(i):
                def step(g):
                    wait = per_group(dve, g)
                    for j in range(2):
                        wait("qk"[i] + "_sq", j + 1)
                        V.tensor_reduce(ss[:, i, j * 32:(j + 1) * 32], sq[j][:].rearrange("p (h d) -> p h d", d=HD),
                                        axis=AX, op=ALU.add).then_inc(sems["ssq"], 1)
                return step

            def head_norm(i):
                dst, name = ((qn, "qn"), (kn, "kn"))[i]

                def step(g):
                    wait = per_group(dve, g)
                    wait("seed2", i + 1)
                    newton(ss[:, i, :], 1.0 / HD, HEAD_EPS, rs[:, i, :], PAIRS * HEADS)
                    for j in range(2):
                        V.tensor_tensor(dst[:, 2 * j:2 * j + 2, :].rearrange("p a (h d) -> p (a h) d", d=HD),
                                        F2[:, j, :].rearrange("p (h d) -> p h d", d=HD),
                                        rs[:, i, 32 * j:32 * j + 32].unsqueeze(2).broadcast_to([P, 32, HD]), ALU.mult)\
                            .then_inc(sems[name], 1)
                return step

            def diagonal_v(p):
                def step(g):
                    wait = per_group(dve, g)
                    wait("v", p + 1)
                    wait("ctx", 0)
                    v = F2[:, p % 2, :].rearrange("p (t h e d) -> p t h e d", t=2, e=2, d=HD)
                    V.tensor_copy(v_diag[0:SEQ, 2 * p:2 * p + 2, :, 0, :], v[0:SEQ, :, :, 0, :])
                    V.tensor_copy(v_diag[SEQ:P, 2 * p, :, 1, :], v[SEQ:P, 1, :, 1, :])
                    V.tensor_copy(v_diag[SEQ:P, 2 * p + 1, :, 1, :], v[SEQ:P, 0, :, 1, :]).then_inc(sems["v_diag"], 1)
                return step

            def subtract_max(p):
                def step(g):
                    wait = per_group(dve, g)
                    wait("s", p + 1)
                    wait("pT", 2 * (p - 1)) if p >= 2 else None
                    wait("s_sub", max(p - 1, 0))
                    S = S4[:, :, 0:256].rearrange("p r (h s) -> p r h s", s=SEQ)
                    four = prob[p % 2][:].rearrange("p (r h) s -> p r h s", r=RT)
                    for i, (a, b) in enumerate(kinds):
                        ins = V.tensor_reduce(mx[:, p % 2, i, :].rearrange("p (r h) -> p r h", r=RT), S[:, :, :, a:b],
                                              axis=AX, op=ALU.max)
                    lk(ins)
                    for i, (a, b) in enumerate(kinds):
                        m = mx[:, p % 2, i, :].rearrange("p (r h) -> p r h", r=RT).unsqueeze(3)
                        ins = V.tensor_tensor(four[:, :, :, a:b], S[:, :, :, a:b],
                                              m.broadcast_to([P, RT, HEADS // RT, b - a]), ALU.subtract)
                    ins.then_inc(sems["s_sub"], 1)
                return step

            def sums(p):
                def step(g):
                    wait = per_group(dve, g)
                    wait("s_exp", p + 1)
                    wait("prob", max(p - 1, 0))
                    for i, (a, b) in enumerate(kinds):
                        ins = V.tensor_reduce(sm[:, p % 2, i, :], prob[p % 2][:, :, a:b], axis=AX, op=ALU.add)
                    lk(ins)
                    V.reciprocal(sm[:, p % 2], sm[:, p % 2]).then_inc(sems["s_rcp"], 1)
                return step

            def ctx_low(j):
                def step(g):
                    wait = per_group(dve, g)
                    wait("c_hi", j + 1)
                    V.tensor_tensor(f_lo[:, :, j * 256:(j + 1) * 256].rearrange("p c (a t) -> p a c t", t=P),
                                    M2[:, 1, :].rearrange("p (a c t) -> p a c t", c=KC, t=P),
                                    f_hi[:, :, j * 256:(j + 1) * 256].bitcast(F32)
                                    .rearrange("p c (a t) -> p a c t", t=P),
                                    ALU.subtract).then_inc(sems["c_lo"], 1)
                return step

            def residual(g):
                wait = per_group(dve, g)
                for j in range(2):
                    wait("o", j + 1)
                    t = x1[:, ds(g * PAIRS + 2 * j, 2), :]
                    ins = V.tensor_tensor(t, S4[:, j, :].rearrange("p (a d) -> p a d", d=D), t, ALU.add)
                lk(ins)
                moments(g, 1, "var2")

            def norm2(g):
                apply_norm(g, 1, per_group(dve, g), "var2", "seed3", "xn2")

            def x2_low(g):
                wait = per_group(dve, g)
                for c in range(KC):
                    wait("x2_hi", c + 1)
                    V.tensor_tensor(f_lo[:, c, :], S4[:, 2 + c, :], f_hi[:, c, :].bitcast(F32), ALU.subtract)\
                        .then_inc(sems["x2_lo"], 1)

            L = M2[:, 0, 0:PAIRS * EXPERTS].rearrange("p (a e) -> p a e", e=EXPERTS)
            wide = [P, PAIRS, EXPERTS]

            def col(i):
                return r1[:, i, :].unsqueeze(2).broadcast_to(wide)

            def router_max(g):
                wait = per_group(dve, g)
                wait("logit", 1)
                wait("c_out", 0)
                lk(V.tensor_reduce(r1[:, 0, :], L, axis=AX, op=ALU.max))
                V.tensor_tensor(rt[:, 0], L, col(0), ALU.subtract).then_inc(sems["l_sub"], 1)

            def router(g):
                wait = per_group(dve, g)
                wait("l_exp", 1)
                e, marked, weight, active, fallback = rt[:, 0], rt[:, 1], rt[:, 2], rt[:, 3], rt[:, 4]
                top, top_w, scaled, is_max, candidate = (r8[:, i] for i in range(5))
                alpha = par[:, PAR_ALPHA:PAR_ALPHA + 1]
                hold()
                for p in range(PAIRS):
                    ins = V.max(top[:, p, :], e[:, p, :])
                lk(ins)
                hold()
                for p in range(PAIRS):
                    ins = V.match_replace(marked[:, p, :], top[:, p, :], e[:, p, :], -1.0)
                lk(V.tensor_reduce(r1[:, 1, :], top, axis=AX, op=ALU.add))
                lk(V.reciprocal(r1[:, 1, :], r1[:, 1, :]))
                in_top = chain.mark(V.tensor_tensor(top_w, top, r1[:, 1, :].unsqueeze(2).broadcast_to([P, PAIRS, TOP_K]),
                                                    ALU.mult))
                all_w = chain.mark(V.tensor_tensor(weight, e, col(1), ALU.mult))
                chain.need(in_top)
                in_top = chain.mark(V.tensor_scalar(scaled, top_w, alpha, None, ALU.mult))
                chain.need(all_w)
                V.tensor_scalar(active, weight, alpha, TAU, ALU.mult, ALU.is_ge)
                chain.need(in_top)
                lk(V.tensor_reduce(r1[:, 2, :], scaled, axis=AX, op=ALU.max))
                in_top = chain.mark(V.tensor_tensor(is_max, scaled, r1[:, 2, :].unsqueeze(2)
                                                    .broadcast_to([P, PAIRS, TOP_K]), ALU.is_equal))
                V.tensor_scalar(r1[:, 3, :], r1[:, 2, :], TAU, None, ALU.is_lt)
                chain.need(in_top)
                in_top = chain.mark(V.tensor_tensor(is_max, is_max, top, ALU.mult))
                V.scalar_tensor_tensor(active, marked, 0.0, active, ALU.is_lt, ALU.mult)
                chain.need(in_top)
                lk(V.tensor_reduce(candidate[:, :, 0:1], is_max, axis=AX, op=ALU.max))
                hold()
                for p in range(PAIRS):
                    ins = V.match_replace(fallback[:, p, :], candidate[:, p, :], e[:, p, :], -1.0)
                lk(ins)
                lk(V.scalar_tensor_tensor(fallback, fallback, 0.0, col(3), ALU.is_lt, ALU.mult))
                lk(V.tensor_tensor(active, active, fallback, ALU.max))
                lk(V.tensor_tensor(active, active, weight, ALU.mult))
                lk(V.tensor_reduce(r1[:, 4, :], active, axis=AX, op=ALU.add))
                lk(V.tensor_scalar(r1[:, 4, :], r1[:, 4, :], 1e-12, None, ALU.max))
                lk(V.reciprocal(r1[:, 4, :], r1[:, 4, :]))
                V.tensor_tensor(combined[:], active, col(4), ALU.mult).then_inc(sems["comb"], 1)

            pipeline(dve, [
                (norm1, True), (subtract_max(0), False), (norm1_apply, True), (sums(0), False),
                (subtract_max(1), False), (x_low, True), (subtract_max(2), False), (sums(1), False),
                (square_sums(0), True), (sums(2), False), (head_norm(0), True), (subtract_max(3), False),
                (ctx_low(0), False), (sums(3), False), (square_sums(1), True), (head_norm(1), True),
                (ctx_low(1), False), (residual, False), (diagonal_v(0), True), (norm2, False),
                (diagonal_v(1), True), (diagonal_v(2), True), (x2_low, False), (diagonal_v(3), True),
                (router_max, False), (router, False)], chain)

        @block.tensor
        def _(pe):
            T = nc.tensor
            pe.wait_ge(s_split_w, 7)

            def split_product(dst, left, right, first, last):
                T.matmul(dst, left[0], right[0], start=first, stop=False)
                T.matmul(dst, left[0], right[1], start=False, stop=False)
                return T.matmul(dst, left[1], right[0], start=False, stop=last)

            def project(dst_banks, bias, w_col, name):
                for j in range(2):
                    if name == "o":
                        wait_o[0]("c_lo", j + 1)
                    for p in (2 * j, 2 * j + 1):
                        dst = dst_banks[:, j, (p % 2) * D:(p % 2 + 1) * D]
                        T.matmul(dst, ones_all[:], b_rows[:, bias:bias + D], start=True, stop=False)
                        for c in range(KC):
                            w = slice(w_col + c * D, w_col + (c + 1) * D)
                            ins = split_product(dst, (f_hi[:, c, p * P:(p + 1) * P], f_lo[:, c, p * P:(p + 1) * P]),
                                                (w_hi[:, w], w_lo[:, w]), False, c == KC - 1)
                    ins.then_inc(sems[name], 1)

            def transposes(wait, name_in, per, src, dst, name_out):
                for c in range(KC):
                    for p in range(PAIRS):
                        if c == 0 and p % per == 0:
                            wait(name_in, p // per + 1)
                        ins = T.transpose(dst[:, c, p * P:(p + 1) * P], src[:, p, c * P:(c + 1) * P], ident)
                    ins.then_inc(sems[name_out], 1)

            def x_transposes(g):
                wait = per_group(pe, g)
                wait("v_diag", 0)
                transposes(wait, "xn", 1, xn, F2, "xT")

            def project_q(g):
                wait = per_group(pe, g)
                wait("x_lo", 2)
                project(F2, B_Q, W_Q, "q")

            def q_transposes(g):
                transposes(per_group(pe, g), "qn", 2, qn, F2, "qT")

            def context(dst, rows, bias, cols):
                T.matmul(dst, ones_kind[:], b_rows[:, bias:bias + D], start=True, stop=False)
                for i, w in enumerate(cols):
                    ins = split_product(dst, (rows(y_hi[i]), rows(y_lo[i])),
                                        (w_hi[:, w:w + D], w_lo[:, w:w + D]), False, i == 1)
                return ins

            def project_k(g):
                wait = per_group(pe, g)
                wait("y_lo", 2)
                wait("qT_sb", 2)
                for j in range(2):
                    for p in (2 * j, 2 * j + 1):
                        ins = context(F2[:, j, (p % 2) * D:(p % 2 + 1) * D],
                                      lambda t: t[:, p, 0:2, :].rearrange("p a s -> p (a s)"), B_K, (W_KM, W_KD))
                    ins.then_inc(sems["k"], 1)

            def k_transposes(g):
                transposes(per_group(pe, g), "kn", 2, kn, F2, "kT")

            def project_v(p):
                def step(g):
                    wait = per_group(pe, g)
                    if p < 2:
                        wait("k_diag", 2)
                    else:
                        wait("v_diag", p - 1)
                    for b in range(2):
                        ins = context(F2[:, p % 2, b * D:(b + 1) * D],
                                      lambda t: t[:, p, b:b + 2, :].rearrange("p a s -> p (a s)"), B_V, (W_VM, W_VD))
                    ins.then_inc(sems["v"], 1)
                return step

            def scores(p):
                def step(g):
                    wait = per_group(pe, g)
                    if p == 0:
                        wait("k_diag", 2)
                        wait("qT_sb", 2)
                        wait("x2_lo", 0)
                    else:
                        wait("s_sub", p)
                    for c in range(KC):
                        for b in range(2):
                            for r in range(RT):
                                t = p * P + b * SEQ
                                f = slice(32 * r, 32 * r + 32)
                                ins = T.matmul(S4[b * SEQ:(b + 1) * SEQ, r, c * P:(c + 1) * P], qT[f, c, t:t + SEQ],
                                               k_diag[f, c, 2 * p + b, :, :].rearrange("p e s -> p (e s)"),
                                               start=True, stop=True)
                    ins.then_inc(sems["s"], 1)
                return step

            def p_transposes(p, j):
                def step(g):
                    wait = per_group(pe, g)
                    if j == 0:
                        wait("prob", p + 1)
                    if p == 0 and j == 0:
                        wait("c_sb", 0)
                    else:
                        wait("pT_sb", 2 * p + j)
                    flat = prob[p % 2][:].rearrange("p h s -> p (h s)")
                    for i in range(4):
                        n = 4 * j + i
                        ins = T.transpose(M2[:, 0, i * P:(i + 1) * P], flat[:, n * P:(n + 1) * P], ident)
                    ins.then_inc(sems["pT"], 1)
                return step

            def attend(p):
                def step(g):
                    wait = per_group(pe, g)
                    if p == 0:
                        wait("v_diag", 4)
                    if p == 2:
                        wait("c_lo", 1)
                    wait("pT_sb", 2 * p + 2)
                    for b in range(2):
                        for n in range(HC):
                            r, c = n // KC, n % KC
                            col = ((p % 2) * KC + c) * P + b * SEQ
                            ins = T.matmul(M2[32 * r:32 * r + 32, 1, col:col + SEQ],
                                           v_diag[:, 2 * p + b, RT * c + r].rearrange("p e d -> p (e d)"),
                                           pT[p % 2][:, n, b * SEQ:(b + 1) * SEQ], start=True, stop=True)
                    ins.then_inc(sems["ctx"], 1)
                return step

            wait_o = [None]

            def project_o(g):
                wait_o[0] = per_group(pe, g)
                wait_o[0]("s_sub", 4)
                project(S4, B_O, W_O, "o")

            def x2_transposes(g):
                transposes(per_group(pe, g), "xn2", 1, xn, S4[:, 2:4, :], "x2T")

            def logits(g):
                wait = per_group(pe, g)
                wait("x2_lo", 2)
                for p in range(PAIRS):
                    dst = M2[:, 0, p * EXPERTS:(p + 1) * EXPERTS]
                    for c in range(KC):
                        w = slice(W_G + c * EXPERTS, W_G + (c + 1) * EXPERTS)
                        t = slice(p * P, (p + 1) * P)
                        ins = split_product(dst, (f_hi[:, c, t], f_lo[:, c, t]), (w_hi[:, w], w_lo[:, w]),
                                            c == 0, c == KC - 1)
                ins.then_inc(sems["logit"], 1)

            def combine(g):
                wait = per_group(pe, g)
                wait("comb", 1)
                for p in range(PAIRS):
                    ins = T.transpose(M2[0:EXPERTS, 1, p * P:(p + 1) * P], combined[:, p, :], ident)
                ins.then_inc(sems["cT"], 1)

            pipeline(pe, [
                (scores(0), False), (scores(1), False), (x_transposes, True), (p_transposes(0, 0), False),
                (scores(2), False), (p_transposes(0, 1), False), (project_q, True), (scores(3), False),
                (attend(0), False), (p_transposes(1, 0), False), (p_transposes(1, 1), False), (attend(1), False),
                (p_transposes(2, 0), False), (q_transposes, True), (p_transposes(2, 1), False), (project_k, True),
                (attend(2), False), (p_transposes(3, 0), False), (p_transposes(3, 1), False), (attend(3), False),
                (k_transposes, True), (project_o, False), (project_v(0), True), (project_v(1), True),
                (project_v(2), True), (x2_transposes, False), (project_v(3), True), (logits, False),
                (combine, False)])

    made = ("gate", "up", "silu", "scaled", "h", "h_hi", "h_lo", "down", "dn_hi", "dn_lo")
    ev = {n: nc.alloc_semaphore(f"e_{n}") for n in made}
    s_cb = [nc.alloc_semaphore(f"e_cb{i}") for i in range(SLOTS)]
    s_dn = [nc.alloc_semaphore(f"e_dn{i}") for i in range(SLOTS)]
    s_split, s_split_lo, s_acc_sb, s_yT, s_y, s_out = (nc.alloc_semaphore(f"e_{n}") for n in
                                                      ("split", "split_lo", "acc_sb", "yT", "y", "out"))
    G8 = [F2[:, 0, :], F2[:, 1, :]]
    U8 = [M2[:, 0, :], M2[:, 1, :]]
    ACC, YT = S4[:, 0:2, :], S4[:, 2:4, :]

    def waits(engine):
        def wait(name, g, j, back=0):
            engine.wait_ge(ev[name], g * CHUNKS + j + (1 + CREDIT - back))
        return wait

    with nc.Block() as block2:

        @block2.sync
        def _(sp):
            for sem in (s_acc_sb, s_yT, s_y, s_out):
                sp.sem_inc(sem, 1)
            with sp.Fori(0, GROUPS) as g:
                def triple(m, wait_free):
                    for r in range(SLOTS):
                        c = g * CHUNKS + m * SLOTS + r
                        if wait_free:
                            sp.wait_ge(ev["scaled"], c + (1 + CREDIT - SLOTS))
                        cut = (96, 64, 32)[r]
                        for e, a, b in ((r, 0, cut), (r + 1, cut, P)):
                            src = c_dram[ds(m * 4 + e, 1), ds(g * GROUP, GROUP)].broadcast_to([b - a, GROUP])
                            sp.dma_start(cb[r][a:b, :], src).then_inc(s_cb[r], 16)
                        sp.wait_ge(ev["dn_lo"], c + (1 + CREDIT - SLOTS))
                        sp.dma_start(dn_raw[r][:], w_down[ds(m * SLOTS + r, 1), :, :].rearrange("a p d -> (a p) d"))\
                            .then_inc(s_dn[r], 16)
                with sp.Fori(0, CHUNKS // SLOTS) as m:
                    triple(m, True)
                sp.wait_ge(s_y, g * 2 + 3)
                sp.dma_start(out[:, ds(g * PAIRS, PAIRS), :], y_out[:]).then_inc(s_out, 16)
            sp.wait_ge(s_out, 16 * GROUPS + 1)

        def run(engine, body, after_group):
            with engine.Fori(0, GROUPS) as g:
                for j in range(CHUNKS):
                    body(g, j, g * (CHUNKS // SLOTS) + (j // SLOTS + 1))
                if after_group:
                    after_group(g)

        @block2.gpsimd
        def _(pool):
            G = nc.gpsimd
            wait = waits(pool)
            for name in ("scaled", "dn_lo"):
                pool.sem_inc(ev[name], CREDIT)

            def body(g, j, fills):
                r = j % SLOTS
                wait("silu", g, j)
                pool.wait_ge(s_cb[r], fills * 32)
                G.tensor_tensor(hid[r][:], hid[r][:], cb[r][:], ALU.mult).then_inc(ev["scaled"], 1)
                wait("dn_hi", g, j)
                wait("down", g, j, SLOTS)
                G.tensor_tensor(dn_lo[r][:], dn_raw[r][:], dn_hi[r][:].bitcast(F32), ALU.subtract)\
                    .then_inc(ev["dn_lo"], 1)

            run(pool, body, None)

        @block2.scalar
        def _(act):
            A = nc.scalar
            wait = waits(act)
            for name in ("silu", "h_hi", "dn_hi"):
                act.sem_inc(ev[name], CREDIT)
            act.wait_ge(s_raw, 64)
            for j in range(0, CHUNKS, 2):
                A.activation(up_hi[:, j:j + 2].rearrange("p a k g f -> p (a k g f)"),
                             up_raw[:, j:j + 2].rearrange("p a k g f -> p (a k g f)"), ACT.Copy).then_inc(s_split, 1)

            def body(g, j, fills):
                r = j % SLOTS
                wait("down", g, j, SLOTS)
                act.wait_ge(s_dn[r], fills * 16)
                A.activation(dn_hi[r][:], dn_raw[r][:], ACT.Copy).then_inc(ev["dn_hi"], 1)
                wait("gate", g, j)
                wait("h_lo", g, j, SLOTS)
                A.activation(hid[r][:], G8[j % 2], ACT.Silu).then_inc(ev["silu"], 1)
                wait("h", g, j)
                wait("down", g, j, 2)
                A.activation(h_hi[j % 2][:], hid[r][:], ACT.Copy).then_inc(ev["h_hi"], 1)

            def after(g):
                wait("down", g, CHUNKS - 1)
                act.wait_ge(s_yT, g * 2 + 1)
                A.activation(acc_sb[:, 0, :], ACC[:, 0, :], ACT.Copy).then_inc(s_acc_sb, 1)

            run(act, body, after)

        @block2.vector
        def _(dve):
            V = nc.vector
            wait = waits(dve)
            for name in ("h", "h_lo"):
                dve.sem_inc(ev[name], CREDIT)
            for j in range(0, CHUNKS, 2):
                dve.wait_ge(s_split, j // 2 + 1)
                V.tensor_tensor(up_lo[:, j:j + 2].rearrange("p a k g f -> p (a k g f)"),
                                up_raw[:, j:j + 2].rearrange("p a k g f -> p (a k g f)"),
                                up_hi[:, j:j + 2].bitcast(F32).rearrange("p a k g f -> p (a k g f)"),
                                ALU.subtract).then_inc(s_split_lo, 1)

            def body(g, j, fills):
                r = j % SLOTS
                wait("scaled", g, j)
                wait("up", g, j)
                V.tensor_tensor(hid[r][:], U8[j % 2], hid[r][:], ALU.mult).then_inc(ev["h"], 1)
                wait("h", g, j)
                wait("h_hi", g, j)
                wait("down", g, j, 2)
                V.tensor_tensor(h_lo[j % 2][:], hid[r][:], h_hi[j % 2][:].bitcast(F32), ALU.subtract)\
                    .then_inc(ev["h_lo"], 1)

            def after(g):
                wait("down", g, CHUNKS - 1)
                dve.wait_ge(s_yT, g * 2 + 1)
                V.tensor_copy(acc_sb[:, 1, :], ACC[:, 1, :]).then_inc(s_acc_sb, 1)
                dve.wait_ge(s_out, g * 16 + 1)
                for i in range(2):
                    dve.wait_ge(s_yT, g * 2 + i + 2)
                    V.tensor_tensor(y_out[:, 2 * i:2 * i + 2, :], YT[:, i, :].rearrange("p (a d) -> p a d", d=D),
                                    x1[:, ds(g * PAIRS + 2 * i, 2), :], ALU.add).then_inc(s_y, 1)

            run(dve, body, after)

        @block2.tensor
        def _(pe):
            T = nc.tensor
            wait = waits(pe)
            for name in ("gate", "up", "down"):
                pe.sem_inc(ev[name], CREDIT)
            pe.wait_ge(s_split_lo, CHUNKS // 2)

            def up(g, j):
                for i, (dst, name, free) in enumerate(((G8[j % 2], "gate", "silu"), (U8[j % 2], "up", "h"))):
                    wait(free, g, j, 2)
                    for c in range(KC):
                        t = ds(g * GROUP, GROUP)
                        hi, lo = up_hi[:, j, c, i, :], up_lo[:, j, c, i, :]
                        T.matmul(dst, hi, x2_hi[:, c, t], start=c == 0, stop=False)
                        T.matmul(dst, hi, x2_lo[:, c, t], start=False, stop=False)
                        ins = T.matmul(dst, lo, x2_hi[:, c, t], start=False, stop=c == KC - 1)
                    ins.then_inc(ev[name], 1)

            def down(g, j):
                first, last = j == 0, j == CHUNKS - 1
                wait("h_lo", g, j)
                wait("dn_lo", g, j)
                r = j % SLOTS
                if first:
                    pe.wait_ge(s_acc_sb, g * 2 + 1)
                for m in range(KC):
                    f = slice(m * P, (m + 1) * P)
                    T.matmul(ACC[:, m, :], dn_hi[r][:, f], h_hi[j % 2][:], start=first, stop=False)
                    T.matmul(ACC[:, m, :], dn_hi[r][:, f], h_lo[j % 2][:], start=False, stop=False)
                    ins = T.matmul(ACC[:, m, :], dn_lo[r][:, f], h_hi[j % 2][:], start=False, stop=last)
                ins.then_inc(ev["down"], 1)

            def body(g, j, fills):
                up(g, j)
                if j >= LAG:
                    down(g, j - LAG)

            def after(g):
                for j in range(CHUNKS - LAG, CHUNKS):
                    down(g, j)
                pe.wait_ge(s_acc_sb, g * 2 + 3)
                pe.wait_ge(s_y, g * 2 + 1)
                for p in range(PAIRS):
                    for m in range(KC):
                        ins = T.transpose(YT[:, p // 2, ((p % 2) * KC + m) * P:((p % 2) * KC + m + 1) * P],
                                          acc_sb[:, m, p * P:(p + 1) * P], ident)
                    if p % 2:
                        ins.then_inc(s_yT, 1)

            run(pe, body, after)


def kernel(**inputs):
    import concourse.bacc as bacc
    from concourse.bass_utils import run_bass_kernel_spmd

    a = {k.replace("L0_xattn_", "").replace("L0_ffn_", ""): np.asarray(v) for k, v in inputs.items()}

    def rows(t, n):
        return t.reshape(n, P, -1).transpose(1, 0, 2).reshape(P, -1)

    kv = np.concatenate([a["Wk"], a["Wv"]], axis=1).reshape(CTX, HEADS, 2, HD)
    b_kv = np.concatenate([a["bk"], a["bv"]]).reshape(HEADS, 2, HD)
    w_attn = np.concatenate([
        rows(a["Wq"], KC), kv[:, :, 0].reshape(CTX, D), a["Wkv_dca"][:, :D],
        kv[:, :, 1].reshape(CTX, D), a["Wkv_dca"][:, D:], rows(a["Wo"], KC), rows(a["gate_weight"].T, KC)], axis=1)
    b_attn = np.zeros((2, 4 * D), np.float32)
    b_attn[0] = np.concatenate([a["bq"], b_kv[:, 0].ravel(), b_kv[:, 1].ravel(), a["bo"]])
    b_attn[1, D:3 * D] = a["bkv_dca"]
    consts = np.zeros((P, C_END), np.float32)
    consts[:, C_ID:C_ID + P] = np.eye(P)
    for p in range(P):
        consts[p, C_ODD + p // HD % 2] = 1
    consts[[0, 32], C_ALL:C_ALL + P] = 1
    for b in range(2):
        consts[[0, 32], C_KIND + b * SEQ:C_KIND + b * SEQ + MAIN] = 1
        consts[[64, 96], C_KIND + b * SEQ + MAIN:C_KIND + (b + 1) * SEQ] = 1
    params = np.zeros((P, PAR_END), np.float32)
    for i, n in enumerate(("qn_w", "qn_b", "kn_w", "kn_b", "kn_dca_w", "kn_dca_b")):
        params[:, i] = np.tile(a[n], HC)
    params[:, PAR_ALPHA] = a["layer_alpha"]
    gu = a["gate_up_proj"].reshape(EXPERTS, 2, INTER, D).transpose(1, 0, 2, 3).reshape(2, CHUNKS, P, KC, P)
    arrays = dict(
        x=a["x"].reshape(TOKENS, D), yT=a["ctx_1024"].reshape(TOKENS, CTX).T, w_attn=w_attn, b_attn=b_attn,
        consts=consts, params=params,
        w_up=gu.transpose(4, 1, 3, 0, 2),
        w_down=a["down_proj"].transpose(0, 2, 1).reshape(CHUNKS, P, D),
    )
    arrays = {n: np.ascontiguousarray(t) for n, t in arrays.items()}
    nc = bacc.Bacc("TRN2", target_bir_lowering=False, num_devices=1)
    aps = {n: nc.dram_tensor(n, t.shape, F32, kind="ExternalInput").ap() for n, t in arrays.items()}
    out = nc.dram_tensor("out", (TOKENS, D), F32, kind="ExternalOutput").ap()
    c_dram = nc.dram_tensor("c_dram", (EXPERTS, TOKENS), F32, kind="Internal").ap()
    aps["x"] = aps["x"].rearrange("(a p) d -> p a d", p=P)
    build(nc, **aps, out=out.rearrange("(a p) d -> p a d", p=P), c_dram=c_dram)
    r = run_bass_kernel_spmd(nc, [arrays], core_ids=[0])
    return r.results[0]["out"].reshape(BATCH, SEQ, D)
```

```python
import numpy as np

import concourse.bass as bass
from concourse import mybir
from concourse.bass import ds

F32 = mybir.dt.float32
F32R = mybir.dt.float32r
ALU = mybir.AluOpType
ACT = mybir.ActivationFunctionType
AX = mybir.AxisListType.X

P = 128
BATCH, SEQ, D = 32, 64, 256
TOKENS = BATCH * SEQ
CTX, DCA = 128, 16
MAIN = SEQ - DCA
HEADS, HD = 16, 16
HC = HEADS // 2
RT = 4
EXPERTS, INTER, TOP_K = 32, 96, 8
TAU = 0.05
LN_EPS, HEAD_EPS = 1e-5, 1e-6
GROUP = 512
GROUPS = TOKENS // GROUP
PAIRS = GROUP // P
KC = D // P
CHUNKS = EXPERTS * INTER // P
SLOTS = 3
CREDIT = 3
LAG = 2
ROUTER_AT = 5
AHEAD_SPLIT = 4

W_Q, B_Q, PART_K = 0, 512, 768
W_KM, W_KD, B_K, PART_V = 768, 1024, 1280, 1536
W_VM, W_VD, B_V, W_O, B_O, W_G, W_END = 1536, 1792, 2048, 2304, 2816, 3072, 3136
C_ID, C_ODD, C_ALL, C_KIND, C_END = 0, 128, 130, 258, 386
PAR_QW, PAR_QB, PAR_K, PAR_ALPHA, PAR_END = 0, 1, 2, 6, 7


def build(nc, x, yT, w_attn, consts, params, w_up, w_down, out, c_dram):
    place = [nc.sbuf_base + (-nc.sbuf_base) % 64]
    top = nc.sbuf_usable_end

    def at(cursor, name, shape, dt=F32):
        size = int(np.prod(shape[1:])) * 4
        t = nc.alloc_sbuf_tensor_at(name, shape, dt, offset=cursor[0])
        cursor[0] += size + (-size) % 32
        assert cursor[0] <= top, (name, cursor[0], top)
        return t

    x2_hi = at(place, "x2_hi", [P, KC, TOKENS], F32R)
    x2_lo = at(place, "x2_lo", [P, KC, TOKENS], F32R)
    x1 = at(place, "x1", [P, GROUPS * PAIRS, D])
    lo_at = [place[0]]
    up_raw = at(place, "up_raw", [P, CHUNKS, KC, 2, P])
    up_lo = at(lo_at, "up_lo", [P, CHUNKS, KC, 2, P], F32R)
    con = at(place, "con", [P, C_END])
    ident = con[:, C_ID:C_ID + P]

    a2 = [place[0]]
    up_hi = at(a2, "up_hi", [P, CHUNKS, KC, 2, P], F32R)
    hid = [at(a2, f"hid{i}", [P, GROUP]) for i in range(SLOTS)]
    h_hi = [at(a2, f"h_hi{i}", [P, GROUP], F32R) for i in range(2)]
    h_lo = [at(a2, f"h_lo{i}", [P, GROUP], F32R) for i in range(2)]
    cb = [at(a2, f"cb{i}", [P, GROUP]) for i in range(SLOTS)]
    dn_raw = [at(a2, f"dn_raw{i}", [P, D]) for i in range(SLOTS)]
    dn_hi = [at(a2, f"dn_hi{i}", [P, D], F32R) for i in range(SLOTS)]
    dn_lo = [at(a2, f"dn_lo{i}", [P, D], F32R) for i in range(SLOTS)]
    acc_sb = at(a2, "acc_sb", [P, KC, GROUP])
    y_out = at(a2, "y_out", [P, PAIRS, D])

    a1 = [place[0]]
    w_hi = at(a1, "w_hi", [P, W_O], F32R)
    w_lo = at(a1, "w_lo", [P, W_O], F32R)
    ones_kind = at(a1, "ones_kind", [P, P], F32R)
    y_raw = at(a1, "y_raw", [P, TOKENS])
    y_hi = [at(a1, f"y_hi{i}", [P, PAIRS, 3, SEQ], F32R) for i in range(2)]
    y_lo = [at(a1, f"y_lo{i}", [P, PAIRS, 3, SEQ], F32R) for i in range(2)]
    xn = at(a1, "xn", [P, PAIRS, D])
    sq = [at(a1, f"sq{i}", [P, 512]) for i in range(2)]
    raw_at = [a1[0]]
    qT = at(a1, "qT", [P, KC, GROUP])
    k_diag = at(a1, "k_diag", [P, KC, 2 * PAIRS, 2, SEQ])
    prob = [at(a1, f"prob{i}", [P, HEADS, SEQ]) for i in range(2)]
    w_raw = at(raw_at, "w_raw", [P, W_END])
    assert raw_at[0] <= a1[0]
    v_diag = at(a1, "v_diag", [P, 2 * PAIRS, HC, 2, HD])
    pT = [at(a1, f"pT{i}", [P, HC, P]) for i in range(2)]
    par_k = at(a1, "par_k", [P, 2, 4])
    ss = at(a1, "ss", [P, 2, PAIRS * HEADS])
    rs = at(a1, "rs", [P, 2, PAIRS * HEADS])
    mx = at(a1, "mx", [P, 2, 2, HEADS])
    sm = at(a1, "sm", [P, 2, 2, HEADS])
    c_first = y_raw[0:EXPERTS, 0:GROUP]

    both = [max(a1[0], a2[0])]
    f_hi = at(both, "f_hi", [P, KC, GROUP], F32R)
    f_lo = at(both, "f_lo", [P, KC, GROUP], F32R)
    kn = at(both, "kn", [P, PAIRS, D])
    wo_hi = at(both, "wo_hi", [P, W_END - W_O], F32R)
    wo_lo = at(both, "wo_lo", [P, W_END - W_O], F32R)
    ones_all = at(both, "ones_all", [P, P], F32R)
    par = at(both, "par", [P, PAR_END])
    eps = at(both, "eps", [P, 2])
    st = at(both, "st", [P, PAIRS, 6])
    mv = at(both, "mv", [P, 2, PAIRS, 2])
    ln = at(both, "ln", [P, 2, PAIRS])
    rl = at(both, "rl", [P, 2, PAIRS])
    nw = at(both, "nw", [P, 3, PAIRS * HEADS])
    rt = at(both, "rt", [P, 5, PAIRS, EXPERTS])
    r8 = at(both, "r8", [P, 5, PAIRS, TOP_K])
    r1 = at(both, "r1", [P, 5, PAIRS])
    combined = at(both, "combined", [P, GROUPS * PAIRS, EXPERTS])
    experts_major = kn[0:EXPERTS, 0:GROUP // D, :].rearrange("p a d -> p (a d)")

    F2 = nc.alloc_psum_tensor("F2", [P, 2, 512], F32)
    M2 = nc.alloc_psum_tensor("M2", [P, 2, 512], F32)
    S4 = nc.alloc_psum_tensor("S4", [P, 4, 512], F32)
    CT = S4[0:EXPERTS, 3, :]
    LATE = S4[:, 2:4, :]
    LAST = GROUPS - 1

    PER = dict(
        x_in=16, var1=1, seed1=1, xn=4, xT=2, x_hi=2, x_lo=2, y_hi=2, y_lo=2, q=2, k=2,
        q_sq=2, k_sq=2, ssq=4, seed2=2, qn=2, kn=2, qT=2, kT=2, qT_sb=2, k_diag=2, v=4, v_diag=4,
        s=4, s_sub=4, s_exp=4, s_rcp=4, prob=4, pT=8, pT_sb=8, ctx=4, c_hi=2, c_lo=2, o=2, res=2, var2=1,
        seed3=1, xn2=4, x2T=2, x2_hi=2, x2_lo=2, logitT=1, logitT_sb=1, logit=1, l_sub=1, l_exp=1, kept=1, comb=1, keep=32,
        dve=0,
    )
    sems = {n: nc.alloc_semaphore(f"s_{n}") for n in PER}
    s_cT, s_c_sb, s_c_out = (nc.alloc_semaphore(n) for n in ("s_cT", "s_c_sb", "s_c_out"))
    s_const, s_y_raw, s_wq, s_w, s_centred, s_w_hi, s_w_lo, s_ones, s_zero_y, s_raw, s_ln, s_hold, s_late_ln, s_late_dve = (
        nc.alloc_semaphore(n) for n in
        ("s_const", "s_y_raw", "s_wq", "s_w", "s_centred", "s_w_hi", "s_w_lo", "s_ones", "s_zero_y", "s_raw", "s_ln",
         "s_hold", "s_late_ln", "s_late_dve"))
    DVE_LINKS = 27

    AHEAD = dict(v=1, s=1, s_sub=1, ctx=1, res=1, l_sub=1, qT=1, v_diag=1 + 1, prob=1, o=1 + 2, keep=1)

    def per_group(engine, g):
        def wait(name, n):
            assert n > 0 or n + AHEAD[name] > 0
            engine.wait_ge(sems[name], g * PER[name] + n + AHEAD.get(name, 0))
        return wait

    def pipeline(engine, steps, *chains, setup={}, late=(), between={}):
        for g in (-2, -1):
            for step, lead in steps:
                if g + lead >= 0:
                    step(g + lead)
                    if g == -2 and step in setup:
                        setup[step]()
        before = [c.n for c in chains]
        with engine.Fori(0, GROUPS - 2) as g:
            for c in chains:
                c.base = g * c.per_round
            for step, lead in steps:
                step(g + lead)
            for c, n in zip(chains, before):
                assert c.n - n == c.per_round, (c.n - n)
        for c, n in zip(chains, before):
            c.base, c.n = 0, n + (GROUPS - 2) * c.per_round
        for g in (GROUPS - 2, GROUPS - 1):
            for step, lead in steps:
                if g + lead < GROUPS and not (g == LAST and step in late):
                    step(g + lead)
                for further, group in between.get((g, step), ()):
                    further(group)

    class Chain:
        def __init__(self, engine, sem, per_round):
            self.engine, self.sem, self.per_round, self.n, self.base = engine, sem, per_round, 0, 0

        def mark(self, ins):
            self.n += 1
            ins.then_inc(self.sem, 1)
            return self.n

        def need(self, n):
            self.engine.wait_ge(self.sem, self.base + n)

        def link(self, ins):
            self.need(self.mark(ins))

    def keep_x2(engine, g):
        per_group(engine, g)("x2_lo", 2)
        for keep, part in ((x2_hi, f_hi), (x2_lo, f_lo)):
            engine.dma_start(keep[:].bitcast(F32)[:, :, ds(g * GROUP, GROUP)], part[:].bitcast(F32))\
                .then_inc(sems["keep"], 16)

    def tensor_steps(pe, o_banks, x2_banks):
        T = nc.tensor

        def split_product(dst, left, right, first, last):
            T.matmul(dst, left[0], right[0], start=first, stop=False)
            T.matmul(dst, left[0], right[1], start=False, stop=False)
            return T.matmul(dst, left[1], right[0], start=False, stop=last)

        def project(dst_banks, bias, w_col, name):
            hi, lo = (wo_hi, wo_lo) if name == "o" else (w_hi, w_lo)
            for j in range(2):
                if name == "o":
                    wait_o[0]("c_lo", j + 1)
                for p in (2 * j, 2 * j + 1):
                    dst = dst_banks[:, j, (p % 2) * D:(p % 2 + 1) * D]
                    T.matmul(dst, ones_all[:], hi[:, bias:bias + D], start=True, stop=False)
                    for c in range(KC):
                        w = slice(w_col + c * D, w_col + (c + 1) * D)
                        ins = split_product(dst, (f_hi[:, c, p * P:(p + 1) * P], f_lo[:, c, p * P:(p + 1) * P]),
                                            (hi[:, w], lo[:, w]), False, c == KC - 1)
                ins.then_inc(sems[name], 1)

        def transposes(wait, name_in, per, src, dst, name_out, free=None):
            for c in range(KC):
                if free:
                    free(c)
                for p in range(PAIRS):
                    if c == 0 and p % per == 0:
                        wait(name_in, p // per + 1)
                    ins = T.transpose(dst[:, c, p * P:(p + 1) * P], src[:, p, c * P:(c + 1) * P], ident)
                ins.then_inc(sems[name_out], 1)

        wait_o = [None]

        def project_o(g):
            wait_o[0] = per_group(pe, g)
            wait_o[0]("s_sub", 4)
            project(o_banks, B_O - W_O, 0, "o")

        def x2_transposes(g):
            transposes(per_group(pe, g), "xn2", 1, kn, x2_banks, "x2T")

        def logits(g):
            wait = per_group(pe, g)
            wait("x2_lo", 2)
            for c in range(KC):
                w = slice(W_G - W_O + c * EXPERTS, W_G - W_O + (c + 1) * EXPERTS)
                ins = split_product(x2_banks[0:EXPERTS, 0, :], (wo_hi[:, w], wo_lo[:, w]),
                                    (f_hi[:, c, :], f_lo[:, c, :]), c == 0, c == KC - 1)
            ins.then_inc(sems["logitT"], 1)

        def logit_transposes(g):
            per_group(pe, g)("logitT_sb", 1)
            pe.sem_inc(s_hold, 1)
            for p in range(PAIRS):
                ins = T.transpose(x2_banks[:, 1, p * EXPERTS:(p + 1) * EXPERTS], experts_major[:, p * P:(p + 1) * P],
                                  ident[0:EXPERTS, 0:EXPERTS])
            ins.then_inc(sems["logit"], 1)

        def combined_transposes(g):
            pe.wait_ge(sems["comb"], g + 1)
            if g:
                pe.wait_ge(s_c_sb, g)
            for p in range(PAIRS):
                ins = T.transpose(CT[:, p * P:(p + 1) * P], combined[:, g * PAIRS + p, :], ident)
            ins.then_inc(s_cT, 1)

        return ((split_product, project, transposes),
                (project_o, x2_transposes, logits, logit_transposes, combined_transposes))

    def scalar_steps(act, lns, x2_banks):
        A = nc.scalar

        def seed(src, tmp, dst, scale, eps_col, name):
            lns.link(A.activation(tmp, src, ACT.Ln, scale=scale, bias=eps[:, eps_col:eps_col + 1]))
            A.activation(dst, tmp, ACT.Exp, scale=-0.5).then_inc(sems[name], 1)

        def seed3(g):
            wait = per_group(act, g)
            wait("var2", 1)
            seed(mv[:, 1, :, 1], ln[:, 1, :], rl[:, 1, :], 1.0, 0, "seed3")

        def x2_high(g):
            wait = per_group(act, g)
            for c in range(KC):
                wait("x2T", c + 1)
                A.activation(f_hi[:, c, :], x2_banks[:, c, :], ACT.Copy).then_inc(sems["x2_hi"], 1)

        def copy_logits(g):
            per_group(act, g)("logitT", 1)
            A.activation(experts_major, x2_banks[0:EXPERTS, 0, :], ACT.Copy).then_inc(sems["logitT_sb"], 1)

        def logit_exp(g):
            wait = per_group(act, g)
            wait("l_sub", 1)
            A.activation(rt[:, 0], rt[:, 0], ACT.Exp).then_inc(sems["l_exp"], 1)

        def copy_combined(g, dst):
            act.wait_ge(s_cT, g + 1)
            A.activation(dst, CT, ACT.Copy).then_inc(s_c_sb, 1)

        return seed, (seed3, x2_high, copy_logits, logit_exp), copy_combined

    def vector_steps(dve, chain, o_banks, x2_banks):
        V = nc.vector
        lk = chain.link

        def hold():
            dve.sem_inc(s_hold, 1)

        def newton(var, scale, e, y, n):
            v, t = nw[:, 1, 0:n], nw[:, 2, 0:n]
            V.tensor_scalar(v, var, scale, e, ALU.mult, ALU.add)
            lk(V.tensor_tensor(t, y, y, ALU.mult))
            lk(V.tensor_tensor(t, t, v, ALU.mult))
            lk(V.tensor_scalar(t, t, -0.5, 1.5, ALU.mult, ALU.add))
            lk(V.tensor_tensor(y, y, t, ALU.mult))

        def moments(g, i, name):
            hold()
            for p in range(PAIRS):
                ins = V.bn_stats(st[:, p, :], x1[:, ds(g * PAIRS + p, 1), :].rearrange("p a d -> p (a d)"))
            lk(ins)
            hold()
            for p in range(PAIRS):
                ins = V.bn_aggr(mv[:, i, p, :], st[:, p, :])
            ins.then_inc(sems[name], 1)

        def apply_norm(dst, g, i, wait, var_name, seed_name, out_name):
            wait(seed_name, 1)
            wait(var_name, 1)
            newton(mv[:, i, :, 1], 1.0, LN_EPS, rl[:, i, :], PAIRS)
            for p in range(PAIRS):
                V.tensor_scalar(dst[:, p, :], x1[:, ds(g * PAIRS + p, 1), :].rearrange("p a d -> p (a d)"),
                                mv[:, i, p, 0:1], rl[:, i, p:p + 1], ALU.subtract, ALU.mult)\
                    .then_inc(sems[out_name], 1)

        def residual(g):
            wait = per_group(dve, g)
            for j in range(2):
                wait("o", j + 1)
                t = x1[:, ds(g * PAIRS + 2 * j, 2), :]
                V.tensor_tensor(t, o_banks[:, j, :].rearrange("p (a d) -> p a d", d=D), t, ALU.add)\
                    .then_inc(sems["res"], 1)
            wait("res", 2)
            moments(g, 1, "var2")

        def norm2(g):
            apply_norm(kn, g, 1, per_group(dve, g), "var2", "seed3", "xn2")

        def x2_low(g):
            wait = per_group(dve, g)
            for c in range(KC):
                wait("x2_hi", c + 1)
                V.tensor_tensor(f_lo[:, c, :], x2_banks[:, c, :], f_hi[:, c, :].bitcast(F32), ALU.subtract)\
                    .then_inc(sems["x2_lo"], 1)

        L = x2_banks[:, 1, 0:PAIRS * EXPERTS].rearrange("p (a e) -> p a e", e=EXPERTS)
        wide = [P, PAIRS, EXPERTS]

        def col(i):
            return r1[:, i, :].unsqueeze(2).broadcast_to(wide)

        def router_max(g):
            wait = per_group(dve, g)
            wait("logit", 1)
            lk(V.tensor_reduce(r1[:, 0, :], L, axis=AX, op=ALU.max))
            V.tensor_tensor(rt[:, 0], L, col(0), ALU.subtract).then_inc(sems["l_sub"], 1)

        marked, weight, active, fallback = rt[:, 1], rt[:, 2], rt[:, 3], rt[:, 4]
        top, top_w, scaled, is_max, candidate = (r8[:, i] for i in range(5))
        alpha = par[:, PAR_ALPHA:PAR_ALPHA + 1]

        def router_keep(g):
            per_group(dve, g)("l_exp", 1)
            V.tensor_copy(combined[:, ds(g * PAIRS, PAIRS), :], rt[:, 0]).then_inc(sems["kept"], 1)

        def of_group(g):
            return combined[:, g * PAIRS:(g + 1) * PAIRS, :]

        def router_top(g):
            e = of_group(g)
            per_group(dve, g)("kept", 1)
            hold()
            for p in range(PAIRS):
                ins = V.max(top[:, p, :], e[:, p, :])
            lk(ins)
            hold()
            for p in range(PAIRS):
                ins = V.match_replace(marked[:, p, :], top[:, p, :], e[:, p, :], -1.0)
            lk(V.tensor_reduce(r1[:, 1, :], top, axis=AX, op=ALU.add))
            lk(V.reciprocal(r1[:, 1, :], r1[:, 1, :]))
            in_top = chain.mark(V.tensor_tensor(top_w, top, r1[:, 1, :].unsqueeze(2).broadcast_to([P, PAIRS, TOP_K]),
                                                ALU.mult))
            all_w = chain.mark(V.tensor_tensor(weight, e, col(1), ALU.mult))
            chain.need(in_top)
            in_top = chain.mark(V.tensor_scalar(scaled, top_w, alpha, None, ALU.mult))
            chain.need(all_w)
            V.tensor_scalar(active, weight, alpha, TAU, ALU.mult, ALU.is_ge)
            chain.need(in_top)

        def router_fallback(g):
            e = of_group(g)
            lk(V.tensor_reduce(r1[:, 2, :], scaled, axis=AX, op=ALU.max))
            in_top = chain.mark(V.tensor_tensor(is_max, scaled, r1[:, 2, :].unsqueeze(2)
                                                .broadcast_to([P, PAIRS, TOP_K]), ALU.is_equal))
            V.tensor_scalar(r1[:, 3, :], r1[:, 2, :], TAU, None, ALU.is_lt)
            chain.need(in_top)
            in_top = chain.mark(V.tensor_tensor(is_max, is_max, top, ALU.mult))
            V.scalar_tensor_tensor(active, marked, 0.0, active, ALU.is_lt, ALU.mult)
            chain.need(in_top)
            lk(V.tensor_reduce(candidate[:, :, 0:1], is_max, axis=AX, op=ALU.max))
            hold()
            for p in range(PAIRS):
                ins = V.match_replace(fallback[:, p, :], candidate[:, p, :], e[:, p, :], -1.0)
            lk(ins)

        def router_weights(g):
            lk(V.scalar_tensor_tensor(fallback, fallback, 0.0, col(3), ALU.is_lt, ALU.mult))
            lk(V.tensor_tensor(active, active, fallback, ALU.max))
            lk(V.tensor_tensor(active, active, weight, ALU.mult))
            lk(V.tensor_reduce(r1[:, 4, :], active, axis=AX, op=ALU.add))
            lk(V.tensor_scalar(r1[:, 4, :], r1[:, 4, :], 1e-12, None, ALU.max))
            lk(V.reciprocal(r1[:, 4, :], r1[:, 4, :]))
            V.tensor_tensor(of_group(g), active, col(4), ALU.mult).then_inc(sems["comb"], 1)

        return ((newton, moments, apply_norm),
                (residual, norm2, x2_low, router_max, router_keep, router_top, router_fallback, router_weights))

    with nc.Block() as block:

        @block.sync
        def _(sp):
            for name, n in AHEAD.items():
                sp.sem_inc(sems[name], n)
            sp.dma_start(x1[:, 0:PAIRS, :], x[:, 0:PAIRS, :]).then_inc(sems["x_in"], 16)
            sp.dma_start(con[:], consts).then_inc(s_const, 16)
            sp.dma_start(par[:], params).then_inc(s_const, 16)
            sp.dma_start(y_raw[:], yT).then_inc(s_y_raw, 16)
            for g in range(1, GROUPS):
                sp.wait_ge(sems["x_in"], 16 * g)
                sp.dma_start(x1[:, g * PAIRS:(g + 1) * PAIRS, :], x[:, g * PAIRS:(g + 1) * PAIRS, :])\
                    .then_inc(sems["x_in"], 16)
            for i in range(4):
                n = CHUNKS // 4
                sp.dma_start(up_raw[:, i * n:(i + 1) * n], w_up[:, i * n:(i + 1) * n]).then_inc(s_raw, 16)
            with sp.Fori(0, LAST) as g:
                keep_x2(sp, g)
            sp.wait_ge(s_c_sb, 1)
            sp.dma_start(c_dram[:, 0:GROUP], c_first).then_inc(s_c_out, 16)
            sp.wait_ge(sems["keep"], 32 * LAST + AHEAD["keep"])

        kinds = ((0, MAIN), (MAIN, SEQ))

        @block.gpsimd
        def _(pool):
            G = nc.gpsimd
            G.memset(v_diag[:], 0.0)
            for t in (*y_hi, *y_lo):
                last = G.memset(t[:].bitcast(F32), 0.0)
            last.then_inc(s_zero_y, 1)
            pool.wait_ge(s_zero_y, 1)
            pool.wait_ge(s_y_raw, 16)

            def context_low(g):
                wait = per_group(pool, g)
                y = y_raw[:, ds(g * GROUP, GROUP)].rearrange("p (a b s) -> p a b s", b=2, s=SEQ)
                for i, (a, b) in enumerate(kinds):
                    wait("y_hi", i + 1)
                    for t, n in ((0, 2), (2, 1)):
                        ins = G.tensor_tensor(y_lo[i][:, :, t:t + n, a:b], y[:, :, 0:n, a:b],
                                              y_hi[i][:, :, t:t + n, a:b].bitcast(F32), ALU.subtract)
                    ins.then_inc(sems["y_lo"], 1)

            def normalise(p):
                def step(g):
                    wait = per_group(pool, g)
                    wait("s_rcp", p + 1)
                    for i, (a, b) in enumerate(kinds):
                        t = prob[p % 2][:, :, a:b]
                        ins = G.tensor_tensor(t, t, sm[:, p % 2, i, :].unsqueeze(2).broadcast_to([P, HEADS, b - a]),
                                              ALU.mult)
                    ins.then_inc(sems["prob"], 1)
                return step

            pipeline(pool, [
                (context_low, 1), (normalise(2), 0), (normalise(3), 0), (normalise(0), 1), (normalise(1), 1)])

        @block.scalar
        def _(act):
            A = nc.scalar
            act.dma_start(w_raw[:, 0:PART_K], w_attn[:, 0:PART_K]).then_inc(s_wq, 16)
            act.dma_start(w_raw[:, PART_K:], w_attn[:, PART_K:]).then_inc(s_w, 16)
            A.preload_act_table_set("natural_log_exp_and_others")
            act.wait_ge(s_const, 32)
            A.activation(ones_all[:], con[:, C_ALL:C_ALL + P], ACT.Copy).then_inc(s_ones, 1)
            A.activation(ones_kind[:], con[:, C_KIND:C_KIND + P], ACT.Copy).then_inc(s_ones, 1)

            def weights_high():
                act.wait_ge(s_centred, 1)
                A.activation(w_hi[:, 0:PART_K], w_raw[:, 0:PART_K], ACT.Copy).then_inc(s_w_hi, 1)
                act.wait_ge(s_w, 16)
                A.activation(w_hi[:, PART_V:], w_raw[:, PART_V:W_O], ACT.Copy)
                A.activation(wo_hi[:], w_raw[:, W_O:], ACT.Copy).then_inc(s_w_hi, 1)
                act.wait_ge(s_centred, 2)
                A.activation(w_hi[:, PART_K:PART_V], w_raw[:, PART_K:PART_V], ACT.Copy).then_inc(s_w_hi, 1)
                act.wait_ge(s_y_raw, 16)
                act.wait_ge(s_zero_y, 1)

            lns = Chain(act, s_ln, 4)
            seed, late, copy_combined = scalar_steps(act, lns, M2)
            seed3, x2_high, copy_logits, logit_exp = late

            def context_high(g):
                wait = per_group(act, g)
                y = y_raw[:, ds(g * GROUP, GROUP)].rearrange("p (a b s) -> p a b s", b=2, s=SEQ)
                wait("v", 0)
                for i, (a, b) in enumerate(kinds):
                    for t, n in ((0, 2), (2, 1)):
                        ins = A.activation(y_hi[i][:, :, t:t + n, a:b], y[:, :, 0:n, a:b], ACT.Copy)
                    ins.then_inc(sems["y_hi"], 1)

            def seed1(g):
                wait = per_group(act, g)
                wait("var1", 1)
                seed(mv[:, 0, :, 1], ln[:, 0, :], rl[:, 0, :], 1.0, 0, "seed1")

            def x_high(g):
                wait = per_group(act, g)
                wait("o", -2)
                for c in range(KC):
                    wait("xT", c + 1)
                    A.activation(f_hi[:, c, :], F2[:, c, :], ACT.Copy).then_inc(sems["x_hi"], 1)

            def squares(i):
                def step(g):
                    wait = per_group(act, g)
                    name = "qk"[i]
                    for j in range(2):
                        wait(name, j + 1)
                        if i:
                            wait("ssq", j + 1)
                        A.activation(sq[j][:], F2[:, j, :], ACT.Square).then_inc(sems[name + "_sq"], 1)
                return step

            def seed2(i):
                def step(g):
                    wait = per_group(act, g)
                    wait("ssq", 2 * i + 2)
                    seed(ss[:, i, :], nw[:, 0, :], rs[:, i, :], 1.0 / HD, 1, "seed2")
                return step

            def queries(g):
                wait = per_group(act, g)
                wait("s", 0)
                for c in range(KC):
                    wait("qT", c + 1)
                    A.activation(qT[:, c, :], F2[:, c, :], ACT.Identity, scale=par[:, PAR_QW:PAR_QW + 1],
                                 bias=par[:, PAR_QB:PAR_QB + 1]).then_inc(sems["qT_sb"], 1)

            def keys(g):
                wait = per_group(act, g)
                for c in range(KC):
                    wait("kT", c + 1)
                    for i, (a, b) in enumerate(kinds):
                        src = F2[:, c, :].rearrange("p (b s) -> p b s", s=SEQ)[:, :, a:b]
                        for e in range(2):
                            ins = A.activation(k_diag[:, c, :, e, a:b], src, ACT.Identity,
                                               scale=par_k[:, e, 2 * i:2 * i + 1], bias=par_k[:, e, 2 * i + 1:2 * i + 2])
                    ins.then_inc(sems["k_diag"], 1)

            def diagonal_v(p):
                def step(g):
                    wait = per_group(act, g)
                    wait("v", p + 1)
                    wait("ctx", 0)
                    v = F2[:, p % 2, :].rearrange("p (t h e d) -> p t h e d", t=2, e=2, d=HD)
                    A.activation(v_diag[0:SEQ, 2 * p:2 * p + 2, :, 0, :], v[0:SEQ, :, :, 0, :], ACT.Copy)
                    A.activation(v_diag[SEQ:P, 2 * p, :, 1, :], v[SEQ:P, 1, :, 1, :], ACT.Copy)
                    A.activation(v_diag[SEQ:P, 2 * p + 1, :, 1, :], v[SEQ:P, 0, :, 1, :], ACT.Copy)\
                        .then_inc(sems["v_diag"], 1)
                return step

            def exps(p):
                def step(g):
                    wait = per_group(act, g)
                    wait("s_sub", p + 1)
                    t = prob[p % 2][:].rearrange("p h s -> p (h s)")
                    A.activation(t, t, ACT.Exp, scale=HD ** -0.5).then_inc(sems["s_exp"], 1)
                return step

            def copy_pT(p, j):
                def step(g):
                    wait = per_group(act, g)
                    wait("ctx", max(p - 1, 0))
                    wait("pT", 2 * p + j + 1)
                    A.activation(pT[p % 2][:, 4 * j:4 * j + 4, :].rearrange("p a b -> p (a b)"),
                                 M2[:, 0, :], ACT.Copy).then_inc(sems["pT_sb"], 1)
                return step

            def ctx_high(j):
                def step(g):
                    wait = per_group(act, g)
                    wait("ctx", 2 * j + 2)
                    wait("keep", 0)
                    A.activation(f_hi[:, :, j * 256:(j + 1) * 256].rearrange("p c (a t) -> p a c t", t=P),
                                 M2[:, 1, :].rearrange("p (a c t) -> p a c t", c=KC, t=P), ACT.Copy)\
                        .then_inc(sems["c_hi"], 1)
                return step

            pipeline(act, [
                (squares(0), 1), (copy_pT(0, 0), 0), (context_high, 1), (copy_pT(0, 1), 0), (seed2(0), 1),
                (copy_pT(1, 0), 0), (exps(2), 0), (copy_pT(1, 1), 0), (queries, 1), (ctx_high(0), 0),
                (exps(3), 0), (squares(1), 1), (copy_pT(2, 0), 0), (seed2(1), 1), (copy_pT(2, 1), 0),
                (copy_pT(3, 0), 0), (seed1, 2), (copy_pT(3, 1), 0), (ctx_high(1), 0), (keys, 1),
                (diagonal_v(0), 1), (diagonal_v(1), 1), (seed3, 0), (diagonal_v(2), 1), (diagonal_v(3), 1),
                (x_high, 2), (exps(0), 1), (x2_high, 0), (copy_logits, 0), (exps(1), 1), (logit_exp, 0)], lns,
                setup={x_high: weights_high}, late=late)
            copy_combined(0, c_first)

        @block.vector
        def _(dve):
            V = nc.vector
            chain = Chain(dve, sems["dve"], DVE_LINKS)
            lk = chain.link
            (newton, moments, apply_norm), late = vector_steps(dve, chain, S4, M2)
            residual, norm2, x2_low, router_max, router_keep, *router = late

            V.memset(r8[:, 4], -3.0)
            V.memset(eps[:, 0:1], LN_EPS)
            V.memset(eps[:, 1:2], HEAD_EPS)
            dve.wait_ge(s_zero_y, 1)

            def centre(a, b):
                n = (b - a) // HD
                v = w_raw[:, a:b].rearrange("p (h d) -> p h d", d=HD)
                mean = ss[:, 0, 0:n]
                lk(V.tensor_reduce(mean, v, axis=AX, op=ALU.add))
                lk(V.tensor_scalar(mean, mean, 1.0 / HD, None, ALU.mult))
                V.tensor_tensor(v, v, mean.unsqueeze(2).broadcast_to([P, n, HD]), ALU.subtract).then_inc(s_centred, 1)

            def weights_low(hi, lo, a, b, made, bias, base=0):
                dve.wait_ge(s_w_hi, made)
                t, c = slice(a - base, b - base), slice(bias - base, bias - base + D)
                lk(V.tensor_tensor(lo[:, t], w_raw[:, a:b], hi[:, t].bitcast(F32), ALU.subtract))
                for r in (32, 96):
                    ins = V.tensor_copy(hi[r:r + 1, c], lo[r:r + 1, c])
                ins.then_inc(s_w_lo, 1)

            def centre_queries():
                dve.wait_ge(s_wq, 16)
                centre(0, PART_K)

            def prepare_weights():
                weights_low(w_hi, w_lo, 0, PART_K, 1, B_Q)
                dve.wait_ge(s_const, 32)
                for e in range(2):
                    V.tensor_scalar(par_k[:, e, :], par[:, PAR_K:PAR_K + 4], con[:, C_ODD + e:C_ODD + e + 1], None,
                                    ALU.mult)
                dve.wait_ge(s_w, 16)
                dve.wait_ge(s_centred, 1)
                centre(PART_K, PART_V)
                weights_low(w_hi, w_lo, PART_V, W_O, 2, B_V)
                weights_low(wo_hi, wo_lo, W_O, W_END, 2, B_O, W_O)
                weights_low(w_hi, w_lo, PART_K, PART_V, 3, B_K)

            def norm1(g):
                wait = per_group(dve, g)
                wait("x_in", 16)
                moments(g, 0, "var1")

            def norm1_apply(g):
                wait = per_group(dve, g)
                wait("qT", 0)
                apply_norm(xn, g, 0, wait, "var1", "seed1", "xn")

            def x_low(c):
                def step(g):
                    wait = per_group(dve, g)
                    wait("x_hi", c + 1)
                    V.tensor_tensor(f_lo[:, c, :], F2[:, c, :], f_hi[:, c, :].bitcast(F32), ALU.subtract)\
                        .then_inc(sems["x_lo"], 1)
                return step

            def square_sums(i):
                def step(g):
                    wait = per_group(dve, g)
                    for j in range(2):
                        wait("qk"[i] + "_sq", j + 1)
                        V.tensor_reduce(ss[:, i, j * 32:(j + 1) * 32], sq[j][:].rearrange("p (h d) -> p h d", d=HD),
                                        axis=AX, op=ALU.add).then_inc(sems["ssq"], 1)
                return step

            def head_norm(i):
                dst, name = ((xn, "qn"), (kn, "kn"))[i]

                def step(g):
                    wait = per_group(dve, g)
                    wait("seed2", i + 1)
                    newton(ss[:, i, :], 1.0 / HD, HEAD_EPS, rs[:, i, :], PAIRS * HEADS)
                    for j in range(2):
                        V.tensor_tensor(dst[:, 2 * j:2 * j + 2, :].rearrange("p a (h d) -> p (a h) d", d=HD),
                                        F2[:, j, :].rearrange("p (h d) -> p h d", d=HD),
                                        rs[:, i, 32 * j:32 * j + 32].unsqueeze(2).broadcast_to([P, 32, HD]), ALU.mult)\
                            .then_inc(sems[name], 1)
                return step

            def keys_read(g):
                per_group(dve, g)("kT", 2)

            def subtract_max(p):
                def step(g):
                    wait = per_group(dve, g)
                    wait("s", p + 1)
                    wait("pT", 2 * (p - 1)) if p >= 2 else None
                    wait("s_sub", max(p - 1, 0))
                    S = S4[:, :, 0:256].rearrange("p r (h s) -> p r h s", s=SEQ)
                    four = prob[p % 2][:].rearrange("p (r h) s -> p r h s", r=RT)
                    for i, (a, b) in enumerate(kinds):
                        ins = V.tensor_reduce(mx[:, p % 2, i, :].rearrange("p (r h) -> p r h", r=RT), S[:, :, :, a:b],
                                              axis=AX, op=ALU.max)
                    lk(ins)
                    for i, (a, b) in enumerate(kinds):
                        m = mx[:, p % 2, i, :].rearrange("p (r h) -> p r h", r=RT).unsqueeze(3)
                        ins = V.tensor_tensor(four[:, :, :, a:b], S[:, :, :, a:b],
                                              m.broadcast_to([P, RT, HEADS // RT, b - a]), ALU.subtract)
                    ins.then_inc(sems["s_sub"], 1)
                return step

            def sums(p):
                def step(g):
                    wait = per_group(dve, g)
                    wait("s_exp", p + 1)
                    wait("prob", max(p - 1, 0))
                    for i, (a, b) in enumerate(kinds):
                        ins = V.tensor_reduce(sm[:, p % 2, i, :], prob[p % 2][:, :, a:b], axis=AX, op=ALU.add)
                    lk(ins)
                    V.reciprocal(sm[:, p % 2], sm[:, p % 2]).then_inc(sems["s_rcp"], 1)
                return step

            def ctx_low(j):
                def step(g):
                    wait = per_group(dve, g)
                    wait("c_hi", j + 1)
                    V.tensor_tensor(f_lo[:, :, j * 256:(j + 1) * 256].rearrange("p c (a t) -> p a c t", t=P),
                                    M2[:, 1, :].rearrange("p (a c t) -> p a c t", c=KC, t=P),
                                    f_hi[:, :, j * 256:(j + 1) * 256].bitcast(F32)
                                    .rearrange("p c (a t) -> p a c t", t=P),
                                    ALU.subtract).then_inc(sems["c_lo"], 1)
                return step

            x_low1 = x_low(1)
            sums_3 = sums(3)
            between = {(LAST, sums_3): [(step, 0) for step in router]}
            pipeline(dve, [
                (norm1, 2), (square_sums(0), 1), (subtract_max(2), 0), (sums(2), 0), (head_norm(0), 1),
                (subtract_max(3), 0), (ctx_low(0), 0), (sums_3, 0), (square_sums(1), 1), (head_norm(1), 1),
                (norm1_apply, 2), (ctx_low(1), 0), (residual, 0), (x_low(0), 2), (keys_read, 1), (norm2, 0),
                (x_low1, 2), (subtract_max(0), 1), (sums(0), 1), (x2_low, 0), (subtract_max(1), 1),
                (router_max, 0), (router_keep, 0), (sums(1), 1)], chain,
                setup={norm1_apply: centre_queries, x_low1: prepare_weights}, late=late, between=between)

        @block.tensor
        def _(pe):
            T = nc.tensor
            pe.wait_ge(s_const, 32)
            (split_product, project, transposes), late = tensor_steps(pe, S4, M2)
            project_o, x2_transposes, logits, logit_transposes, combined_transposes = late

            def query_weights():
                pe.wait_ge(s_ones, 2)
                pe.wait_ge(s_w_lo, 1)

            def other_weights():
                pe.wait_ge(s_w_lo, 4)

            def x_transposes(g):
                wait = per_group(pe, g)
                transposes(wait, "xn", 1, xn, F2, "xT", lambda c: wait("v_diag", c - 1))

            def project_q(g):
                wait = per_group(pe, g)
                wait("x_lo", 2)
                project(F2, B_Q, W_Q, "q")

            def q_transposes(g):
                transposes(per_group(pe, g), "qn", 2, xn, F2, "qT")

            def context(dst, rows, bias, cols):
                T.matmul(dst, ones_kind[:], w_hi[:, bias:bias + D], start=True, stop=False)
                for i, w in enumerate(cols):
                    ins = split_product(dst, (rows(y_hi[i]), rows(y_lo[i])),
                                        (w_hi[:, w:w + D], w_lo[:, w:w + D]), False, i == 1)
                return ins

            def project_k(g):
                wait = per_group(pe, g)
                wait("y_lo", 2)
                for j in range(2):
                    wait("qT_sb", j + 1)
                    for p in (2 * j, 2 * j + 1):
                        ins = context(F2[:, j, (p % 2) * D:(p % 2 + 1) * D],
                                      lambda t: t[:, p, 0:2, :].rearrange("p a s -> p (a s)"), B_K, (W_KM, W_KD))
                    ins.then_inc(sems["k"], 1)

            def k_transposes(g):
                transposes(per_group(pe, g), "kn", 2, kn, F2, "kT")

            def project_v(p):
                def step(g):
                    wait = per_group(pe, g)
                    if p < 2:
                        wait("k_diag", p + 1)
                    else:
                        wait("v_diag", p - 1)
                    for b in range(2):
                        ins = context(F2[:, p % 2, b * D:(b + 1) * D],
                                      lambda t: t[:, p, b:b + 2, :].rearrange("p a s -> p (a s)"), B_V, (W_VM, W_VD))
                    ins.then_inc(sems["v"], 1)
                return step

            def scores(p):
                def step(g):
                    wait = per_group(pe, g)
                    if p == 0:
                        wait("k_diag", 2)
                        wait("qT_sb", 2)
                        wait("res", 0)
                    else:
                        wait("s_sub", p)
                    for c in range(KC):
                        for b in range(2):
                            for r in range(RT):
                                t = p * P + b * SEQ
                                f = slice(32 * r, 32 * r + 32)
                                ins = T.matmul(S4[b * SEQ:(b + 1) * SEQ, r, c * P:(c + 1) * P], qT[f, c, t:t + SEQ],
                                               k_diag[f, c, 2 * p + b, :, :].rearrange("p e s -> p (e s)"),
                                               start=True, stop=True)
                    ins.then_inc(sems["s"], 1)
                return step

            def p_transposes(p, j):
                def step(g):
                    wait = per_group(pe, g)
                    if j == 0:
                        wait("prob", p + 1)
                    if p == 0 and j == 0:
                        wait("l_sub", 0)
                    else:
                        wait("pT_sb", 2 * p + j)
                    flat = prob[p % 2][:].rearrange("p h s -> p (h s)")
                    for i in range(4):
                        n = 4 * j + i
                        ins = T.transpose(M2[:, 0, i * P:(i + 1) * P], flat[:, n * P:(n + 1) * P], ident)
                    ins.then_inc(sems["pT"], 1)
                return step

            def attend(p):
                def step(g):
                    wait = per_group(pe, g)
                    if p == 0:
                        wait("v_diag", 4)
                    if p == 2:
                        wait("c_lo", 1)
                    wait("pT_sb", 2 * p + 2)
                    for b in range(2):
                        for n in range(HC):
                            r, c = n // KC, n % KC
                            col = ((p % 2) * KC + c) * P + b * SEQ
                            ins = T.matmul(M2[32 * r:32 * r + 32, 1, col:col + SEQ],
                                           v_diag[:, 2 * p + b, RT * c + r].rearrange("p e d -> p (e d)"),
                                           pT[p % 2][:, n, b * SEQ:(b + 1) * SEQ], start=True, stop=True)
                    ins.then_inc(sems["ctx"], 1)
                return step

            pipeline(pe, [
                (p_transposes(0, 0), 0), (scores(2), 0), (p_transposes(0, 1), 0), (p_transposes(1, 0), 0),
                (attend(0), 0), (p_transposes(1, 1), 0), (scores(3), 0), (q_transposes, 1), (attend(1), 0),
                (project_k, 1), (p_transposes(2, 0), 0), (p_transposes(2, 1), 0), (p_transposes(3, 0), 0),
                (attend(2), 0), (p_transposes(3, 1), 0), (k_transposes, 1), (attend(3), 0), (project_o, 0),
                (project_v(0), 1), (project_v(1), 1), (project_v(2), 1), (project_v(3), 1), (x_transposes, 2),
                (scores(0), 1), (project_q, 2), (x2_transposes, 0), (scores(1), 1), (logits, 0),
                (logit_transposes, 0)],
                setup={x_transposes: query_weights, project_q: other_weights}, late=late)
            pe.wait_ge(sems["s_sub"], 4 * GROUPS + AHEAD["s_sub"])
            combined_transposes(0)

    made = ("gate", "up", "silu", "scaled", "h", "h_hi", "h_lo", "down", "dn_hi", "dn_lo")
    ev = {n: nc.alloc_semaphore(f"e_{n}") for n in made}
    s_cb = [nc.alloc_semaphore(f"e_cb{i}") for i in range(SLOTS)]
    s_dn = [nc.alloc_semaphore(f"e_dn{i}") for i in range(SLOTS)]
    s_split, s_split_lo, s_acc_sb, s_yT, s_y, s_out = (nc.alloc_semaphore(f"e_{n}") for n in
                                                      ("split", "split_lo", "acc_sb", "yT", "y", "out"))
    G8 = [F2[:, 0, :], F2[:, 1, :]]
    U8 = [M2[:, 0, :], M2[:, 1, :]]
    ACC, YT = S4[:, 0:2, :], S4[:, 2:4, :]

    def waits(engine):
        def wait(name, g, j, back=0):
            engine.wait_ge(ev[name], g * CHUNKS + j + (1 + CREDIT - back))
        return wait

    with nc.Block() as block2:

        @block2.sync
        def _(sp):
            for sem in (s_acc_sb, s_yT, s_y, s_out):
                sp.sem_inc(sem, 1)

            def loads(g):
                sp.wait_ge(s_c_out, g * 16 + 16)
                sp.sem_inc(s_hold, 1)

                def triple(m):
                    for r in range(SLOTS):
                        c = g * CHUNKS + m * SLOTS + r
                        sp.wait_ge(ev["scaled"], c + (1 + CREDIT - SLOTS))
                        cut = (96, 64, 32)[r]
                        for e, a, b in ((r, 0, cut), (r + 1, cut, P)):
                            src = c_dram[ds(m * 4 + e, 1), ds(g * GROUP, GROUP)].broadcast_to([b - a, GROUP])
                            sp.dma_start(cb[r][a:b, :], src).then_inc(s_cb[r], 16)
                        sp.wait_ge(ev["dn_lo"], c + (1 + CREDIT - SLOTS))
                        sp.dma_start(dn_raw[r][:], w_down[ds(m * SLOTS + r, 1), :, :].rearrange("a p d -> (a p) d"))\
                            .then_inc(s_dn[r], 16)
                with sp.Fori(0, CHUNKS // SLOTS) as m:
                    triple(m)

            loads(0)
            with sp.Fori(1, GROUPS) as g:
                loads(g)
            sp.wait_ge(s_out, 16 * GROUPS + 1)

        def run(engine, body, finish, late={}):
            def chunks(g, first):
                for j in range(CHUNKS):
                    body(g, j, g * (CHUNKS // SLOTS) + (j // SLOTS + 1), first)
                    for step, group in (late.get(j, ()) if first else ()):
                        step(group)
                    if not first and j in (LAG - 1, LAG, LAG + 2):
                        finish(g - 1, j, False)
            chunks(0, True)
            with engine.Fori(1, GROUPS) as g:
                chunks(g, False)
            for j in (LAG - 2, LAG - 1, LAG, LAG + 2):
                finish(GROUPS - 1, j, True)

        @block2.gpsimd
        def _(pool):
            G = nc.gpsimd
            wait = waits(pool)
            for name in ("scaled", "dn_lo"):
                pool.sem_inc(ev[name], CREDIT)

            def body(g, j, fills, first):
                r = j % SLOTS
                wait("silu", g, j)
                pool.wait_ge(s_cb[r], fills * 32)
                G.tensor_tensor(hid[r][:], hid[r][:], cb[r][:], ALU.mult).then_inc(ev["scaled"], 1)
                wait("dn_hi", g, j)
                wait("down", g, j, SLOTS)
                G.tensor_tensor(dn_lo[r][:], dn_raw[r][:], dn_hi[r][:].bitcast(F32), ALU.subtract)\
                    .then_inc(ev["dn_lo"], 1)

            run(pool, body, lambda g, j, last: None)

        @block2.scalar
        def _(act):
            A = nc.scalar
            wait = waits(act)
            for name in ("silu", "h_hi", "dn_hi"):
                act.sem_inc(ev[name], CREDIT)
            act.wait_ge(s_raw, 64)

            def split_high(j):
                if j < CHUNKS:
                    A.activation(up_hi[:, j].rearrange("p k g f -> p (k g f)"),
                                 up_raw[:, j].rearrange("p k g f -> p (k g f)"), ACT.Copy).then_inc(s_split, 1)

            for j in range(AHEAD_SPLIT):
                split_high(j)
            _, (seed3, x2_high, copy_logits, logit_exp), copy_combined = scalar_steps(act, Chain(act, s_late_ln, 1), LATE)
            seed3(LAST)
            act.wait_ge(s_c_out, 16)
            A.preload_act_table_set("silu_and_others")

            def body(g, j, fills, first):
                r = j % SLOTS
                wait("down", g, j, SLOTS)
                act.wait_ge(s_dn[r], fills * 16)
                A.activation(dn_hi[r][:], dn_raw[r][:], ACT.Copy).then_inc(ev["dn_hi"], 1)
                wait("gate", g, j)
                wait("h_lo", g, j, SLOTS)
                A.activation(hid[r][:], G8[j % 2], ACT.Silu).then_inc(ev["silu"], 1)
                wait("h", g, j)
                wait("down", g, j, 2)
                A.activation(h_hi[j % 2][:], hid[r][:], ACT.Copy).then_inc(ev["h_hi"], 1)
                if first:
                    split_high(j + AHEAD_SPLIT)

            def finish(g, j, last):
                if j == LAG - 1:
                    wait("down", g, CHUNKS - 1)
                    act.wait_ge(s_yT, g * 2 + 1)
                    A.activation(acc_sb[:, 0, :], ACC[:, 0, :], ACT.Copy).then_inc(s_acc_sb, 1)
                if j == LAG + 2:
                    act.wait_ge(s_y, g * 2 + 3)
                    act.dma_start(out[:, ds(g * PAIRS, PAIRS), :], y_out[:]).then_inc(s_out, 16)

            def store_combined(g):
                if g > 1:
                    act.wait_ge(s_c_out, 16 * g)
                copy_combined(g, experts_major)
                act.wait_ge(s_c_sb, g + 1)
                act.dma_start(c_dram[:, g * GROUP:(g + 1) * GROUP], experts_major).then_inc(s_c_out, 16)

            steps = {2: [(x2_high, LAST)], 3: [(lambda g: keep_x2(act, g), LAST)],
                     4: [(copy_logits, LAST)], 7: [(logit_exp, LAST)]}
            for g in range(1, GROUPS):
                steps[ROUTER_AT + 6 * g] = [(store_combined, g)]
            run(act, body, finish, steps)

        @block2.vector
        def _(dve):
            V = nc.vector
            wait = waits(dve)
            for name in ("h", "h_lo"):
                dve.sem_inc(ev[name], CREDIT)

            def split_low(j):
                if j < CHUNKS:
                    dve.wait_ge(s_split, j + 1)
                    V.tensor_tensor(up_lo[:, j].rearrange("p k g f -> p (k g f)"),
                                    up_raw[:, j].rearrange("p k g f -> p (k g f)"),
                                    up_hi[:, j].bitcast(F32).rearrange("p k g f -> p (k g f)"),
                                    ALU.subtract).then_inc(s_split_lo, 1)

            for j in range(2):
                split_low(j)
            _, (residual, *late) = vector_steps(dve, Chain(dve, s_late_dve, 0), LATE, LATE)
            residual(LAST)
            for j in range(2, AHEAD_SPLIT):
                split_low(j)

            def body(g, j, fills, first):
                r = j % SLOTS
                wait("scaled", g, j)
                wait("up", g, j)
                V.tensor_tensor(hid[r][:], U8[j % 2], hid[r][:], ALU.mult).then_inc(ev["h"], 1)
                wait("h", g, j)
                wait("h_hi", g, j)
                wait("down", g, j, 2)
                V.tensor_tensor(h_lo[j % 2][:], hid[r][:], h_hi[j % 2][:].bitcast(F32), ALU.subtract)\
                    .then_inc(ev["h_lo"], 1)
                if first:
                    split_low(j + AHEAD_SPLIT)

            def finish(g, j, last):
                if j == LAG - 1:
                    wait("down", g, CHUNKS - 1)
                    dve.wait_ge(s_yT, g * 2 + 1)
                    V.tensor_copy(acc_sb[:, 1, :], ACC[:, 1, :]).then_inc(s_acc_sb, 1)
                if j == LAG:
                    dve.wait_ge(s_out, g * 16 + 1)
                    for i in range(2):
                        dve.wait_ge(s_yT, g * 2 + i + 2)
                        V.tensor_tensor(y_out[:, 2 * i:2 * i + 2, :], YT[:, i, :].rearrange("p (a d) -> p a d", d=D),
                                        x1[:, ds(g * PAIRS + 2 * i, 2), :], ALU.add).then_inc(s_y, 1)

            norm2, x2_low, router_max, router_keep, *router = late
            steps = {0: [(norm2, LAST)], 2: [(x2_low, LAST)], 6: [(router_max, LAST)], 8: [(router_keep, LAST)]}
            for g in range(1, GROUPS):
                for i, step in enumerate(router):
                    steps[ROUTER_AT + 6 * (g - 1) + 2 * i] = [(step, g)]
            run(dve, body, finish, steps)

        @block2.tensor
        def _(pe):
            T = nc.tensor
            wait = waits(pe)
            for name in ("gate", "up", "down"):
                pe.sem_inc(ev[name], CREDIT)

            def up(g, j):
                for i, (dst, name, free) in enumerate(((G8[j % 2], "gate", "silu"), (U8[j % 2], "up", "h"))):
                    wait(free, g, j, 2)
                    for c in range(KC):
                        t = ds(g * GROUP, GROUP)
                        hi, lo = up_hi[:, j, c, i, :], up_lo[:, j, c, i, :]
                        T.matmul(dst, hi, x2_hi[:, c, t], start=c == 0, stop=False)
                        T.matmul(dst, hi, x2_lo[:, c, t], start=False, stop=False)
                        ins = T.matmul(dst, lo, x2_hi[:, c, t], start=False, stop=c == KC - 1)
                    ins.then_inc(ev[name], 1)

            def down(g, j):
                first, last = j == 0, j == CHUNKS - 1
                wait("h_lo", g, j)
                wait("dn_lo", g, j)
                r = j % SLOTS
                if first:
                    pe.wait_ge(s_acc_sb, g * 2 + 1)
                for m in range(KC):
                    f = slice(m * P, (m + 1) * P)
                    T.matmul(ACC[:, m, :], dn_hi[r][:, f], h_hi[j % 2][:], start=first, stop=False)
                    T.matmul(ACC[:, m, :], dn_hi[r][:, f], h_lo[j % 2][:], start=False, stop=False)
                    ins = T.matmul(ACC[:, m, :], dn_lo[r][:, f], h_hi[j % 2][:], start=False, stop=last)
                ins.then_inc(ev["down"], 1)

            def body(g, j, fills, first):
                if first:
                    pe.wait_ge(s_split_lo, j + 1)
                up(g, j)
                if j >= LAG:
                    down(g, j - LAG)
                elif not first:
                    down(g - 1, CHUNKS + j - LAG)

            def finish(g, j, last):
                if last and j < LAG:
                    down(g, CHUNKS + j - LAG)
                if j == LAG:
                    pe.wait_ge(s_acc_sb, g * 2 + 3)
                    pe.wait_ge(s_y, g * 2 + 1)
                    for p in range(PAIRS):
                        for m in range(KC):
                            ins = T.transpose(YT[:, p // 2, ((p % 2) * KC + m) * P:((p % 2) * KC + m + 1) * P],
                                              acc_sb[:, m, p * P:(p + 1) * P], ident)
                        if p % 2:
                            ins.then_inc(s_yT, 1)

            _, (project_o, x2_transposes, logits, logit_transposes, combined_transposes) = tensor_steps(pe, LATE, LATE)
            project_o(LAST)
            steps = {2: [(x2_transposes, LAST)], 4: [(logits, LAST)], 6: [(logit_transposes, LAST)],
                     CHUNKS - 1: [(lambda g: pe.wait_ge(sems["keep"], 32 * GROUPS + AHEAD["keep"]), LAST)]}
            for g in range(1, GROUPS):
                steps[ROUTER_AT + 6 * g] = [(combined_transposes, g)]
            run(pe, body, finish, steps)


def kernel(**inputs):
    import concourse.bacc as bacc
    from concourse.bass_utils import run_bass_kernel_spmd

    a = {k.replace("L0_xattn_", "").replace("L0_ffn_", ""): np.asarray(v) for k, v in inputs.items()}

    def rows(t, n):
        return t.reshape(n, P, -1).transpose(1, 0, 2).reshape(P, -1)

    kv = np.concatenate([a["Wk"], a["Wv"]], axis=1).reshape(CTX, HEADS, 2, HD)
    b_kv = np.concatenate([a["bk"], a["bv"]]).reshape(HEADS, 2, HD)

    def bias(main, dca=0.0):
        t = np.zeros((P, D), np.float32)
        t[[0, 32]], t[[64, 96]] = main, dca
        return t

    w_attn = np.concatenate([
        rows(a["Wq"], KC), bias(a["bq"]),
        kv[:, :, 0].reshape(CTX, D), a["Wkv_dca"][:, :D], bias(b_kv[:, 0].ravel(), a["bkv_dca"][:D]),
        kv[:, :, 1].reshape(CTX, D), a["Wkv_dca"][:, D:], bias(b_kv[:, 1].ravel(), a["bkv_dca"][D:]),
        rows(a["Wo"], KC), bias(a["bo"]), rows(a["gate_weight"].T, KC)], axis=1)
    consts = np.zeros((P, C_END), np.float32)
    consts[:, C_ID:C_ID + P] = np.eye(P)
    for p in range(P):
        consts[p, C_ODD + p // HD % 2] = 1
    consts[[0, 32], C_ALL:C_ALL + P] = 1
    for b in range(2):
        consts[[0, 32], C_KIND + b * SEQ:C_KIND + b * SEQ + MAIN] = 1
        consts[[64, 96], C_KIND + b * SEQ + MAIN:C_KIND + (b + 1) * SEQ] = 1
    params = np.zeros((P, PAR_END), np.float32)
    for i, n in enumerate(("qn_w", "qn_b", "kn_w", "kn_b", "kn_dca_w", "kn_dca_b")):
        params[:, i] = np.tile(a[n], HC)
    params[:, PAR_ALPHA] = a["layer_alpha"]
    gu = a["gate_up_proj"].reshape(EXPERTS, 2, INTER, D).transpose(1, 0, 2, 3).reshape(2, CHUNKS, P, KC, P)
    arrays = dict(
        x=a["x"].reshape(TOKENS, D), yT=a["ctx_1024"].reshape(TOKENS, CTX).T, w_attn=w_attn,
        consts=consts, params=params,
        w_up=gu.transpose(4, 1, 3, 0, 2),
        w_down=a["down_proj"].transpose(0, 2, 1).reshape(CHUNKS, P, D),
    )
    arrays = {n: np.ascontiguousarray(t) for n, t in arrays.items()}
    nc = bacc.Bacc("TRN2", target_bir_lowering=False, num_devices=1)
    aps = {n: nc.dram_tensor(n, t.shape, F32, kind="ExternalInput").ap() for n, t in arrays.items()}
    out = nc.dram_tensor("out", (TOKENS, D), F32, kind="ExternalOutput").ap()
    c_dram = nc.dram_tensor("c_dram", (EXPERTS, TOKENS), F32, kind="Internal").ap()
    aps["x"] = aps["x"].rearrange("(a p) d -> p a d", p=P)
    build(nc, **aps, out=out.rearrange("(a p) d -> p a d", p=P), c_dram=c_dram)
    r = run_bass_kernel_spmd(nc, [arrays], core_ids=[0])
    return r.results[0]["out"].reshape(BATCH, SEQ, D)
```
